# Optimizing a Trainium2 kernel written in Bass

```python
import numpy as np
import jax
import jax.numpy as jnp

def _softmax(x, axis=-1):
    return jax.nn.softmax(x, axis=axis)

def _gelu(x):
    return jax.nn.gelu(x, approximate=True)

def _silu(x):
    return jax.nn.silu(x)

def _sigmoid(x):
    return jax.nn.sigmoid(x)

def _layernorm(x, axis=-1, eps=1e-05):
    m = jnp.mean(x, axis=axis, keepdims=True)
    v = jnp.var(x, axis=axis, keepdims=True)
    return (x - m) / jnp.sqrt(v + eps)

def _scatter_add(tgt, idx, src, axis=0):
    return tgt.at[idx].add(src)

def _segment_sum(src, seg, n):
    return jax.ops.segment_sum(src, seg, n)
kernel_name = 'mk_flamingo_gated_d1_seqx_r2_7ab65c'

def setup_inputs(seed: int=0):
    np.random.seed(seed)
    _w = jnp.asarray

    def _rec_inputs():
        import jax
        import jax.numpy as jnp
        _rk = jax.random.key(seed)
        x = -0.0002928 + 1 * jax.random.normal(jax.random.fold_in(_rk, 1), (4, 1024, 512), jnp.float32)
        _lenS = 1024 - jax.random.randint(jax.random.fold_in(_rk, 7), (4,), 0, max(1, 1024 // 4) + 1, jnp.int32)
        _lenS2 = 2048 - jax.random.randint(jax.random.fold_in(_rk, 8), (4,), 0, max(1, 2048 // 4) + 1, jnp.int32)
        _ctx_1024P = jax.random.normal(jax.random.fold_in(_rk, 11), (4, 16, 512), jnp.float32)
        _ctx_1024c = jax.random.dirichlet(jax.random.fold_in(_rk, 511), 0.3 * jnp.ones((16,), jnp.float32), (4, 2048))
        _ctx_1024t = jnp.einsum('bsk,bkd->bsd', _ctx_1024c, _ctx_1024P)
        _ctx_1024t = _ctx_1024t * jax.lax.rsqrt(jnp.mean(jnp.square(_ctx_1024t)) + 1e-12) * 0.953939
        ctx_1024 = -1.39393e-06 + 0.999914 * (_ctx_1024t + 0.3 * jax.random.normal(jax.random.fold_in(_rk, 611), (4, 2048, 512), jnp.float32))
        _validS = jnp.arange(1024)[None, :] < _lenS[:, None]
        _validS2 = jnp.arange(2048)[None, :] < _lenS2[:, None]
        _causal = jnp.tril(jnp.ones((1024, 1024), dtype=bool))
        mask_BxS2_ik0 = jnp.where(jnp.broadcast_to(_validS2[:, :], (4, 2048)), 0, 1).astype(jnp.int32)
        _g = jax.random.normal(jax.random.fold_in(_rk, 9001), (2, 1), jnp.float32)
        _g = jnp.sign(_g) * jnp.maximum(jnp.abs(_g), 1.0) + (_g == 0) * 1.0
        g_xattn = _g[0]
        g_ffn = _g[1]
        return (x, ctx_1024, mask_BxS2_ik0, g_xattn, g_ffn)
    x, ctx_1024, mask_BxS2_ik0, g_xattn, g_ffn = _rec_inputs()

    def _L0_xattn_setup():
        import jax, jax.numpy as jnp
        import numpy as np
        B, SQ, SKV, D, H = (2, 1024, 1024, 512, 16)
        W = D // H

        def _heads(x):
            b, s, _ = x.shape
            return x.reshape(b, s, H, W).transpose(0, 2, 1, 3)
        key = jax.random.key(seed)
        ks = jax.random.split(key, 10)
        s = 1.0 / np.sqrt(D)
        return {'x_q': jax.random.normal(ks[0], (B, SQ, D), jnp.float32), 'x_k': jax.random.normal(ks[1], (B, SKV, D), jnp.float32), 'x_v': jax.random.normal(ks[2], (B, SKV, D), jnp.float32), 'mask': jax.random.randint(ks[3], (B, SKV), 0, 2, jnp.int32), 'Wq': jax.random.normal(ks[4], (D, D), jnp.float32) * s, 'bq': jnp.zeros((D,), jnp.float32), 'Wk': jax.random.normal(ks[5], (D, D), jnp.float32) * s, 'bk': jnp.zeros((D,), jnp.float32), 'Wv': jax.random.normal(ks[6], (D, D), jnp.float32) * s, 'bv': jnp.zeros((D,), jnp.float32)}
    _L0_xattn_all = _L0_xattn_setup()
    _L0_xattn_in = {k: v for k, v in _L0_xattn_all.items() if k in ('Wq', 'bq', 'Wk', 'bk', 'Wv', 'bv')}
    del _L0_xattn_all

    def _L0_ffn_setup():
        import jax, jax.numpy as jnp
        import numpy as np
        D_MODEL, D_FF, D2, DL = (512, 2048, 64, 64)
        D1 = D_FF // D2
        BATCH, SEQ = (2, 512)
        KERNEL_SCALE = D2 ** 0.5
        key = jax.random.key(seed)
        ks = jax.random.split(key, 7)
        xav = lambda k, shape, fan: jax.random.normal(k, shape, jnp.float32) * (2.0 / sum(fan)) ** 0.5
        x = jax.random.normal(ks[0], (BATCH, SEQ, D_MODEL), jnp.float32)
        m1 = xav(ks[1], (D_MODEL, DL), (D_MODEL, DL))
        m2 = xav(ks[2], (DL, D1, D2), (DL, D_FF))
        mb = jax.random.normal(ks[3], (D1, D2), jnp.float32)
        w1 = xav(ks[4], (D_MODEL, D1, D2), (D_MODEL, D_FF))
        w2 = xav(ks[5], (D2, D1, D_MODEL), (D_FF, D_MODEL)) * KERNEL_SCALE
        b2 = jax.random.normal(ks[6], (D_MODEL,), jnp.float32)
        return {'x': x, 'm1': m1, 'm2': m2, 'mb': mb, 'w1': w1, 'w2': w2, 'b2': b2}
    _L0_ffn_all = _L0_ffn_setup()
    _L0_ffn_in = {k: v for k, v in _L0_ffn_all.items() if k in ('m1', 'm2', 'mb', 'w1', 'w2', 'b2')}
    del _L0_ffn_all
    return {'x': x, 'ctx_1024': ctx_1024, 'mask_BxS2_ik0': mask_BxS2_ik0, 'g_xattn': g_xattn, 'g_ffn': g_ffn, 'L0_xattn_Wq': _L0_xattn_in['Wq'], 'L0_xattn_bq': _L0_xattn_in['bq'], 'L0_xattn_Wk': _L0_xattn_in['Wk'], 'L0_xattn_bk': _L0_xattn_in['bk'], 'L0_xattn_Wv': _L0_xattn_in['Wv'], 'L0_xattn_bv': _L0_xattn_in['bv'], 'L0_ffn_m1': _L0_ffn_in['m1'], 'L0_ffn_m2': _L0_ffn_in['m2'], 'L0_ffn_mb': _L0_ffn_in['mb'], 'L0_ffn_w1': _L0_ffn_in['w1'], 'L0_ffn_w2': _L0_ffn_in['w2'], 'L0_ffn_b2': _L0_ffn_in['b2']}

def reference(x, ctx_1024, mask_BxS2_ik0, g_xattn, g_ffn, L0_xattn_Wq, L0_xattn_bq, L0_xattn_Wk, L0_xattn_bk, L0_xattn_Wv, L0_xattn_bv, L0_ffn_m1, L0_ffn_m2, L0_ffn_mb, L0_ffn_w1, L0_ffn_w2, L0_ffn_b2):
    import jax
    import jax.numpy as jnp

    def _L0_xattn_ref(x_q, x_k, x_v, mask, Wq, bq, Wk, bk, Wv, bv):
        import jax, jax.numpy as jnp
        import numpy as np
        B, SQ, SKV, D, H = (2, 1024, 1024, 512, 16)
        W = D // H

        def _heads(x):
            b, s, _ = x.shape
            return x.reshape(b, s, H, W).transpose(0, 2, 1, 3)
        q = _heads(x_q @ Wq.T + bq)
        k = _heads(x_k @ Wk.T + bk)
        v = _heads(x_v @ Wv.T + bv)
        scores = jnp.einsum('bhqw,bhkw->bhqk', q, k) / np.sqrt(W).astype(np.float32)
        m = mask[:, None, None, :].astype(scores.dtype)
        scores = scores - 10000.0 * (1.0 - m)
        p = jax.nn.softmax(scores, axis=-1)
        h = jnp.einsum('bhqk,bhkw->bhqw', p, v)
        return h.transpose(0, 2, 1, 3).reshape(x_q.shape[0], x_q.shape[1], D)

    def _L0_ffn_ref(x, m1, m2, mb, w1, w2, b2):
        import jax, jax.numpy as jnp
        import numpy as np
        D_MODEL, D_FF, D2, DL = (512, 2048, 64, 64)
        D1 = D_FF // D2
        BATCH, SEQ = (2, 512)
        KERNEL_SCALE = D2 ** 0.5
        x_shape = x.shape
        xf = x.reshape(-1, x_shape[-1])
        d1 = w1.shape[1]
        lr = xf @ m1
        mask_logits = jnp.einsum('bl,lxy->bxy', lr, m2) + mb
        quant_mask = jnp.argmax(mask_logits, axis=-1)
        w1p = jnp.transpose(w1, (1, 2, 0))
        w2p = jnp.transpose(w2, (1, 0, 2))
        j = jnp.arange(d1)[None, :]
        w = w1p[j, quant_mask]
        mid = jnp.einsum('ai,aji->aj', xf, w)
        relu = jax.nn.relu(mid)
        v = w2p[j, quant_mask]
        res = jnp.einsum('ai,aij->aj', relu, v) + b2
        return res.reshape(x_shape)
    x = x + jnp.tanh(g_xattn[0]) * _L0_xattn_ref(_layernorm(x, axis=-1), ctx_1024, ctx_1024, mask_BxS2_ik0, L0_xattn_Wq, L0_xattn_bq, L0_xattn_Wk, L0_xattn_bk, L0_xattn_Wv, L0_xattn_bv)
    x = x + jnp.tanh(g_ffn[0]) * _L0_ffn_ref(_layernorm(x, axis=-1), L0_ffn_m1, L0_ffn_m2, L0_ffn_mb, L0_ffn_w1, L0_ffn_w2, L0_ffn_b2)
    return x

_drawn_inputs = setup_inputs


def setup_inputs(seed=0):
    import zlib

    import numpy as np

    out = dict(_drawn_inputs(seed))
    spreads = {'L0_xattn_bq': (0.0, 0.1), 'L0_xattn_bk': (0.0, 0.1), 'L0_xattn_bv': (0.0, 0.1)}
    factors = {}
    for name, (base, spread) in spreads.items():
        noise = np.random.default_rng([zlib.crc32(name.encode()), seed]).standard_normal(out[name].shape)
        drawn = base * np.exp(spread * noise) if base else spread * noise
        out[name] = jnp.asarray(drawn.astype(out[name].dtype))
    for name, factor in factors.items():
        out[name] = (out[name] * factor).astype(out[name].dtype)
    return out
```

```python
from contextlib import ExitStack

import concourse.bass as bass
from concourse import mybir

F32 = mybir.dt.float32
F16 = mybir.dt.float16
I32 = mybir.dt.int32
ACT = mybir.ActivationFunctionType
ALU = mybir.AluOpType
AX_X = mybir.AxisListType.X

P = 128
B, SQ, SKV, D, H = 4, 1024, 2048, 512, 16
W = D // H
SCALE = float(W) ** -0.5
MASKED = 10000.0
EPS = 1e-5
D1, D2 = 32, 64
DFF = D1 * D2
DL = 64
KT = D // P
FT = DFF // P
N = 512
BANKS = 8
HG = P // W
GROUPS = H // HG
UNITS = B * GROUPS
QC = SQ // N
CC = SKV // N
JT = SKV // P
ST = N // P
LN_STEPS = 10


def positive(value):
    return not isinstance(value, int) or value > 0


def vector_layer_norm(dve, n, rows, out, stats, moments, small, sqrt_done, step):
    base = LN_STEPS * n
    var_eps, root, inv, tmp, rstd = (small[:, k, :] for k in range(5))
    total, gap, mean = (moments[:, k, :] for k in range(3))
    for s in range(ST):
        last = dve.bn_stats(stats[:, s, :], rows[:, s, :])
    last.then_inc(step, 1)
    dve.wait_ge(step, base + 1)
    dve.tensor_tensor(total, stats[:, :, 1], stats[:, :, 4], ALU.add)
    dve.tensor_tensor(gap, stats[:, :, 1], stats[:, :, 4], ALU.subtract)
    dve.tensor_tensor(tmp, stats[:, :, 2], stats[:, :, 5], ALU.add).then_inc(step, 1)
    dve.wait_ge(step, base + 2)
    dve.tensor_scalar(mean, total, 0.5, None, ALU.mult)
    dve.tensor_tensor(inv, gap, gap, ALU.mult)
    dve.tensor_scalar(rstd, tmp, 1.0 / D, EPS, ALU.mult, ALU.add).then_inc(step, 1)
    dve.wait_ge(step, base + 3)
    dve.scalar_tensor_tensor(var_eps, inv, 0.25, rstd, ALU.mult, ALU.add).then_inc(step, 1)
    dve.wait_ge(sqrt_done, n + 1)
    dve.reciprocal(inv, root).then_inc(step, 1)
    dve.wait_ge(step, base + 5)
    dve.tensor_tensor(tmp, inv, inv, ALU.mult).then_inc(step, 1)
    dve.wait_ge(step, base + 6)
    dve.tensor_tensor(rstd, tmp, var_eps, ALU.mult).then_inc(step, 1)
    dve.wait_ge(step, base + 7)
    dve.tensor_scalar(tmp, rstd, -0.5, 1.5, ALU.mult, ALU.add).then_inc(step, 1)
    dve.wait_ge(step, base + 8)
    dve.tensor_tensor(rstd, inv, tmp, ALU.mult).then_inc(step, 1)
    dve.wait_ge(step, base + 9)
    for s in range(ST):
        last = dve.tensor_scalar(out[:, s, :], rows[:, s, :], mean[:, s:s + 1], rstd[:, s:s + 1],
                                 ALU.subtract, ALU.mult)
    last.then_inc(step, 1)


def scalar_layer_norm(act, n, small, sqrt_done, step):
    act.wait_ge(step, LN_STEPS * n + 4)
    act.activation(small[:, 1, :], small[:, 0, :], ACT.Sqrt).then_inc(sqrt_done, 1)


def pair_product(pe, out, left, right, tiles=range(KT), start=True, stop=True):
    for k in tiles:
        (lh, ll), (rh, rl) = left(k), right(k)
        pe.matmul(out, lh, rh, start=start and k == tiles[0], stop=False)
        pe.matmul(out, lh, rl, start=False, stop=False)
        last = pe.matmul(out, ll, rh, start=False, stop=stop and k == tiles[-1])
    return last


def project(nc, ident, banks, x, ctxT, mask, WqT, WkT, WvT, bq, bk, bv, s_K, s_Q, s_V, s_mask):
    with ExitStack() as ctx:
        def sb(name, shape, dt):
            return ctx.enter_context(nc.sbuf_tensor(name, shape, dt))

        def sem(name):
            return ctx.enter_context(nc.semaphore(name))

        w_f = [sb(f"w{n}_f", [P, KT, D], F32) for n in "qkv"]
        w_h = [sb(f"w{n}_h", [P, KT, D], F16) for n in "qkv"]
        w_l = [sb(f"w{n}_l", [P, KT, D], F16) for n in "qkv"]
        bq_f = sb("bq_f", [P, KT], F32)
        bq_s = sb("bq_s", [P, KT], F32)
        bk_f = sb("bk_f", [P, KT], F32)
        bv_f = sb("bv_f", [P, D], F32)
        mask_i = sb("mask_i", [UNITS, SKV], I32)
        mask_h = sb("mask_h", [UNITS, SKV], F16)
        ctx_f = sb("ctx_f", [P, 2, KT, N], F32)
        ctx_h = sb("ctx_h", [P, 2, KT, N], F16)
        ctx_l = sb("ctx_l", [P, 2, KT, N], F16)
        k_h = sb("k_h", [P, 2, KT, N], F16)
        k_l = sb("k_l", [P, 2, KT, N], F16)
        v_f = sb("v_f", [P, 2, ST, D], F32)
        x_f = sb("x_f", [P, QC, ST, D], F32)
        xn = sb("xn", [P, ST, D], F32)
        xT_h = sb("xT_h", [P, KT, N], F16)
        xT_l = sb("xT_l", [P, KT, N], F16)
        q_h = sb("q_h", [P, QC, KT, N], F16)
        q_l = sb("q_l", [P, QC, KT, N], F16)
        stats = sb("stats", [P, ST, 6], F32)
        moments = sb("moments", [P, 3, ST], F32)
        small = sb("small", [P, 5, ST], F32)

        weights_loaded = sem("weights_loaded")
        consts_loaded = sem("consts_loaded")
        wq_scaled = sem("wq_scaled")
        weights_hi = sem("weights_hi")
        weights_ready = sem("weights_ready")
        mask_ready = sem("mask_ready")
        mask_stored = sem("mask_stored")
        ctx_loaded = [sem(f"ctx_loaded{i}") for i in range(2)]
        ctx_hi_done = sem("ctx_hi_done")
        ctx_lo_done = sem("ctx_lo_done")
        x_loaded = [sem(f"x_loaded{i}") for i in range(QC)]
        ln_step = sem("ln_step")
        sqrt_done = sem("sqrt_done")
        bank_filled = sem("bank_filled")
        hi_done = sem("hi_done")
        bank_free = sem("bank_free")
        kv_stored = [sem(f"kv_stored{i}") for i in range(2)]
        q_stored = [sem(f"q_stored{i}") for i in range(QC)]
        ident_zero = sem("ident_zero")
        ident_ready = sem("ident_ready")

        JOBS = [("KV", 0), ("T", 0), ("KV", 1), ("Q", 0), ("T", 1), ("KV", 2), ("Q", 1), ("KV", 3)]
        SIZE = {"KV": KT + ST, "T": KT, "Q": KT}
        HIS = KT
        first, at = {}, 0
        for job in JOBS:
            first[job] = at
            at += SIZE[job[0]]
        PER = at
        assert PER % BANKS == 0
        KV_DMAS = 2 + GROUPS

        def through(b, job):
            return PER * b + (first[job] + SIZE[job[0]])

        def before_T(b, c):
            return through(b, ("Q", 0)) if c else through(b - 1, ("Q", 1))

        with nc.Block() as block:
            @block.sync
            def _(sp):
                for f, w in zip(w_f, (WqT, WkT, WvT)):
                    sp.dma_start(f[:], w.rearrange("(k p) o -> p k o", p=P)).then_inc(weights_loaded, 16)
                sp.dma_start(bq_f[:], bq).then_inc(consts_loaded, 16)
                sp.dma_start(bk_f[:], bk).then_inc(consts_loaded, 16)
                sp.dma_start(bv_f[:], bv.partition_broadcast(P)).then_inc(consts_loaded, 16)
                sp.dma_start(mask_i[:], mask).then_inc(consts_loaded, 16)
                sp.wait_ge(mask_ready, 1)
                sp.dma_start(s_mask, mask_h[:]).then_inc(mask_stored, 16)

                def batch(b):
                    for kind, c in JOBS:
                        if kind == "KV":
                            sp.wait_ge(bank_free, through(b, (kind, c)))
                            for s_k, k in zip(s_K, (k_h, k_l)):
                                sp.dma_start(
                                    s_k[bass.ds(b * D, D), c * N:(c + 1) * N].rearrange("(m p) t -> p m t", p=P),
                                    k[:, c % 2]).then_inc(kv_stored[c % 2], 16)
                            for g in range(GROUPS):
                                sp.dma_start(
                                    s_V[bass.ds(b * (GROUPS * SKV) + (g * SKV + c * N), N), :].rearrange(
                                        "(s p) e -> p s e", p=P),
                                    v_f[:, c % 2, :, g * P:(g + 1) * P]).then_inc(kv_stored[c % 2], 16)
                        if kind == "Q":
                            sp.wait_ge(bank_free, through(b, (kind, c)))
                            for s_q, q in zip(s_Q, (q_h, q_l)):
                                sp.dma_start(
                                    s_q[bass.ds(b * D, D), c * N:(c + 1) * N].rearrange("(m p) t -> p m t", p=P),
                                    q[:, c]).then_inc(q_stored[c], 16)

                batch(0)
                with sp.Fori(1, B) as b:
                    batch(b)
                sp.wait_ge(mask_stored, 16)
                for i in range(2):
                    sp.wait_ge(kv_stored[i], 16 * KV_DMAS * B * CC // 2)
                    sp.wait_ge(q_stored[i], 16 * 2 * B)

            @block.gpsimd
            def _(pool):
                def load_ctx(b, c):
                    need = CC * b + (c - 1)
                    if positive(need):
                        pool.wait_ge(ctx_lo_done, need)
                    pool.dma_start(ctx_f[:, c % 2],
                                   ctxT[bass.ds(b * D, D), c * N:(c + 1) * N].rearrange("(k p) t -> p k t", p=P)
                                   ).then_inc(ctx_loaded[c % 2], 16)

                def load_x(b, c):
                    need = LN_STEPS * (QC * b + (c - 1))
                    if positive(need):
                        pool.wait_ge(ln_step, need)
                    pool.dma_start(x_f[:, c], x[bass.ds(b * SQ + c * N, N), :].rearrange("(s p) d -> p s d", p=P)
                                   ).then_inc(x_loaded[c], 16)

                def batch(b):
                    load_ctx(b, 0)
                    load_x(b, 0)
                    load_ctx(b, 1)
                    load_x(b, 1)
                    for c in range(CC):
                        pool.wait_ge(ctx_hi_done, CC * b + (c + 1))
                        pool.tensor_tensor(ctx_l[:, c % 2], ctx_f[:, c % 2], ctx_h[:, c % 2], ALU.subtract
                                           ).then_inc(ctx_lo_done, 1)
                        if c + 2 < CC:
                            load_ctx(b, c + 2)

                pool.memset(ident[:], 0.0).then_inc(ident_zero, 1)
                pool.wait_ge(ident_zero, 1)
                pool.affine_select(out=ident[:], in_=ident[:], compare_op=ALU.not_equal, fill=1.0, base=0,
                                   pattern=[[-1, P]], channel_multiplier=1).then_inc(ident_ready, 1)
                batch(0)
                with pool.Fori(1, B) as b:
                    batch(b)

            @block.scalar
            def _(act):
                def ctx_hi(b, c):
                    act.wait_ge(ctx_loaded[c % 2], 32 * b + 16 * (c // 2 + 1))
                    need = through(b, ("KV", c - 2)) if c >= 2 else through(b - 1, ("KV", c + 2))
                    if positive(need):
                        act.wait_ge(bank_filled, need)
                    act.activation(ctx_h[:, c % 2], ctx_f[:, c % 2], ACT.Copy).then_inc(ctx_hi_done, 1)

                def batch(b):
                    ctx_hi(b, 0)
                    scalar_layer_norm(act, QC * b, small, sqrt_done, ln_step)
                    ctx_hi(b, 1)
                    for kind, c in JOBS:
                        for g in range(HIS):
                            if g == 0 and kind == "KV":
                                need = 16 * KV_DMAS * (2 * b + c // 2)
                                if positive(need):
                                    act.wait_ge(kv_stored[c % 2], need)
                            if g == 0 and kind == "Q":
                                need = 32 * b
                                if positive(need):
                                    act.wait_ge(q_stored[c], need)
                            if g == 0 and kind == "T":
                                need = before_T(b, c)
                                if positive(need):
                                    act.wait_ge(bank_filled, need)
                            n = first[(kind, c)] + g
                            src = banks[:, n % BANKS, :]
                            act.wait_ge(bank_filled, PER * b + (n + 1))
                            if kind == "KV":
                                ins = act.activation(k_h[:, c % 2, g, :], src, ACT.Identity, bias=bk_f[:, g:g + 1])
                            elif kind == "Q":
                                ins = act.activation(q_h[:, c, g, :], src, ACT.Identity, bias=bq_s[:, g:g + 1])
                            else:
                                ins = act.activation(xT_h[:, g, :], src, ACT.Copy)
                            ins.then_inc(hi_done, 1)
                        if (kind, c) == ("T", 0):
                            scalar_layer_norm(act, QC * b + 1, small, sqrt_done, ln_step)
                        if kind == "KV" and c < 2:
                            ctx_hi(b, c + 2)

                for n in range(3):
                    if n == 0:
                        act.wait_ge(wq_scaled, 2)
                    else:
                        act.wait_ge(weights_loaded, 48)
                    act.activation(w_h[n][:], w_f[n][:], ACT.Copy).then_inc(weights_hi, 1)
                act.wait_ge(consts_loaded, 64)
                batch(0)
                with act.Fori(1, B) as b:
                    batch(b)

            @block.vector
            def _(dve):
                def norm(b, c):
                    dve.wait_ge(x_loaded[c], 16 * b + 16)
                    need = through(b, ("T", 0)) if c else through(b - 1, ("T", 1))
                    if positive(need):
                        dve.wait_ge(bank_filled, need)
                    vector_layer_norm(dve, QC * b + c, x_f[:, c], xn, stats, moments, small, sqrt_done, ln_step)

                def batch(b):
                    norm(b, 0)
                    for j, (kind, c) in enumerate(JOBS):
                        for g in range(SIZE[kind]):
                            n = first[(kind, c)] + g
                            src = banks[:, n % BANKS, :]
                            if g < HIS:
                                dve.wait_ge(hi_done, HIS * len(JOBS) * b + (HIS * j + g + 1))
                            else:
                                if g == HIS:
                                    need = 16 * KV_DMAS * (2 * b + c // 2)
                                    if positive(need):
                                        dve.wait_ge(kv_stored[c % 2], need)
                                dve.wait_ge(bank_filled, PER * b + (n + 1))
                            if kind == "KV" and g < HIS:
                                ins = dve.scalar_tensor_tensor(k_l[:, c % 2, g, :], src, bk_f[:, g:g + 1],
                                                               k_h[:, c % 2, g, :], ALU.add, ALU.subtract)
                            elif kind == "KV":
                                ins = dve.tensor_tensor(v_f[:, c % 2, g - HIS, :], src, bv_f[:], ALU.add)
                            elif kind == "Q":
                                ins = dve.scalar_tensor_tensor(q_l[:, c, g, :], src, bq_s[:, g:g + 1],
                                                               q_h[:, c, g, :], ALU.add, ALU.subtract)
                            else:
                                ins = dve.tensor_tensor(xT_l[:, g, :], src, xT_h[:, g, :], ALU.subtract)
                            ins.then_inc(bank_free, 1)
                        if (kind, c) == ("T", 0):
                            norm(b, 1)

                dve.wait_ge(weights_loaded, 48)
                dve.tensor_scalar(w_f[0][:], w_f[0][:], SCALE, None, ALU.mult).then_inc(wq_scaled, 1)
                dve.wait_ge(consts_loaded, 64)
                dve.tensor_scalar(bq_s[:], bq_f[:], SCALE, None, ALU.mult).then_inc(wq_scaled, 1)
                dve.tensor_scalar(mask_h[:], mask_i[:], MASKED, -MASKED, ALU.mult, ALU.add).then_inc(mask_ready, 1)
                for n in range(3):
                    dve.wait_ge(weights_hi, n + 1)
                    dve.tensor_tensor(w_l[n][:], w_f[n][:], w_h[n][:], ALU.subtract).then_inc(weights_ready, 1)
                dve.wait_ge(wq_scaled, 2)
                batch(0)
                with dve.Fori(1, B) as b:
                    batch(b)

            @block.tensor
            def _(pe):
                def weight(n, cols):
                    return lambda k: (w_h[n][:, k, cols], w_l[n][:, k, cols])

                def batch(b):
                    for kind, c in JOBS:
                        if kind == "KV":
                            pe.wait_ge(ctx_lo_done, CC * b + (c + 1))
                        elif kind == "T":
                            pe.wait_ge(ln_step, LN_STEPS * (QC * b + (c + 1)))
                        else:
                            pe.wait_ge(bank_free, through(b, ("T", c)))
                        for g in range(SIZE[kind]):
                            n = first[(kind, c)] + g
                            bank = banks[:, n % BANKS, :]
                            need = PER * b + (n + 1 - BANKS)
                            if positive(need):
                                pe.wait_ge(bank_free, need)
                            if kind == "KV" and g < HIS:
                                last = pair_product(pe, bank, weight(1, slice(g * P, (g + 1) * P)),
                                                    lambda k: (ctx_h[:, c % 2, k, :], ctx_l[:, c % 2, k, :]))
                            elif kind == "KV":
                                rows = slice((g - HIS) * P, (g - HIS + 1) * P)
                                last = pair_product(pe, bank,
                                                    lambda k: (ctx_h[:, c % 2, k, rows], ctx_l[:, c % 2, k, rows]),
                                                    weight(2, slice(0, D)))
                            elif kind == "Q":
                                last = pair_product(pe, bank, weight(0, slice(g * P, (g + 1) * P)),
                                                    lambda k: (xT_h[:, k, :], xT_l[:, k, :]))
                            else:
                                for s in range(ST):
                                    last = pe.transpose(bank[:, s * P:(s + 1) * P], xn[:, s, g * P:(g + 1) * P],
                                                        ident[:])
                            last.then_inc(bank_filled, 1)

                pe.wait_ge(weights_ready, 3)
                pe.wait_ge(ident_ready, 1)
                batch(0)
                with pe.Fori(1, B) as b:
                    batch(b)


def attend(nc, ident, banks, s_K, s_Q, s_V, s_mask, s_heads, w1, w2, w1_h, w1_l, w2_h, w2_l):
    HI0, HI1, LO, MASK_ROW, ONE_ROW, ROWS = 0, W, 2 * W, 3 * W, 3 * W + 1, 3 * W + 2
    STEPS = 2 * QC
    TURNS = UNITS // 2
    PAIRS = JT // 2
    PER = STEPS * PAIRS
    ITEMS = HG * ST * CC
    SLOTS = ITEMS + 1
    TURN_AT = 2
    AHEAD = 2 * PAIRS
    UNIT_DMAS = 3 + 3 * QC + HG + 2
    with ExitStack() as ctx:
        def sb(name, shape, dt):
            return ctx.enter_context(nc.sbuf_tensor(name, shape, dt))

        def sem(name):
            return ctx.enter_context(nc.semaphore(name))

        K = sb("K_stack", [ROWS, 2, HG, SKV], F16)
        Q = sb("Q_stack", [ROWS, 2, QC, HG * N], F16)
        V = sb("V", [P, 2, JT, P], F32)
        probs = sb("probs", [P, 2, 2, HG, N], F32)
        pair_sum = sb("pair_sum", [P, 2, HG, N], F32)
        ones = sb("ones", [P, W], F32)
        maxima = sb("maxima", [P, 2, ITEMS], F32)
        neg_max = sb("neg_max", [P, 2, P], F32)
        shift = sb("shift", [P, 2, P], F16)
        o_raw = sb("o_raw", [P, 2, N], F32)
        rden = sb("rden", [P, 2, N], F32)
        heads = sb("heads", [P, 2, N], F32)
        w_stage = sb("w_stage", [P, 2, DFF], F32)

        consts_ready = sem("b_consts_ready")
        unit_loaded = [sem(f"unit_loaded{i}") for i in range(2)]
        slot_filled = sem("slot_filled")
        slot_free = sem("slot_free")
        neg_max_ready = sem("neg_max_ready")
        shift_loaded = [sem(f"shift_loaded{i}") for i in range(2)]
        scores_ready = sem("scores_ready")
        exp_done = sem("exp_done")
        pv_done = sem("pv_done")
        pair_sum_done = sem("pair_sum_done")
        den_done = sem("den_done")
        o_copied = sem("o_copied")
        rden_done = sem("rden_done")
        heads_ready = sem("heads_ready")
        heads_stored = [sem(f"heads_stored{i}") for i in range(2)]
        w_loaded = [sem(f"w_loaded{i}") for i in range(2)]
        w_hi_done = sem("w_hi_done")
        w_lo_done = sem("w_lo_done")

        RT = DFF // D
        pieces = [(w1[k * P:(k + 1) * P, :], w1_h[:, k, :], w1_l[:, k, :]) for k in range(KT)]
        pieces += [(w2[k * RT * P:(k + 1) * RT * P, :].rearrange("(f p) d -> p f d", p=P),
                    w2_h[:, RT * k:RT * (k + 1), :].rearrange("p f d -> p (f d)"),
                    w2_l[:, RT * k:RT * (k + 1), :].rearrange("p f d -> p (f d)")) for k in range(FT // RT)]

        def slot_runs(s, p):
            start = SLOTS * (s + 1) + AHEAD + 8 * p + (p > 0)
            return [divmod(n, SLOTS) for n in range(start, start + 8 + (p == 0))]

        def slots_of(s, p, last):
            return [(t, k) for t, k in slot_runs(s, p) if not last or t < STEPS or (t == STEPS and k == TURN_AT)]

        def item_of(k):
            item = k if k < TURN_AT else k - 1
            return item // (ST * CC), item // CC % ST, item % CC

        def turns(eng, body):
            body(0, False)
            with eng.Fori(1, TURNS - 1) as i:
                body(i, False)
            body(TURNS - 1, True)

        OPENING = [(0, k) for k in range(SLOTS)] + [(1, k) for k in range(AHEAD)]

        def slot_number(i, t, k):
            skipped = TURN_AT if isinstance(i, int) and i == TURNS - 1 and t == STEPS else 0
            return SLOTS * STEPS * i + (SLOTS * t + k - skipped)

        with nc.Block() as block:
            @block.sync
            def _(sp):
                def load_unit(i, u):
                    need = PER * i + (u - 1) * (PER // 2)
                    if positive(need):
                        sp.wait_ge(pv_done, need)
                    buf, got = u % 2, unit_loaded[u % 2]
                    rows = bass.ds(i * (2 * P) + u * P, P)
                    for at, s_k in ((HI0, s_K[0]), (HI1, s_K[0]), (LO, s_K[1])):
                        sp.dma_start(K[at:at + W, buf], s_k[rows, :].rearrange("(h w) t -> w h t", w=W)).then_inc(got, 16)
                    for at, s_q in ((HI0, s_Q[0]), (HI1, s_Q[1]), (LO, s_Q[0])):
                        for c in range(QC):
                            sp.dma_start(Q[at:at + W, buf, c, :].rearrange("w (h t) -> w h t", h=HG),
                                         s_q[rows, c * N:(c + 1) * N].rearrange("(h w) t -> w h t", w=W)
                                         ).then_inc(got, 16)
                    for h in range(HG):
                        sp.dma_start(K[MASK_ROW:MASK_ROW + 1, buf, h, :], s_mask[bass.ds(i * 2 + u, 1), :]
                                     ).then_inc(got, 16)
                    half = SKV // 2
                    for k in range(2):
                        sp.dma_start(V[:, buf, k * JT // 2:(k + 1) * JT // 2, :],
                                     s_V[bass.ds(i * (2 * SKV) + (u * SKV + k * half), half), :].rearrange(
                                         "(j p) e -> p j e", p=P)).then_inc(got, 16)

                def load_shift(i, t):
                    sp.wait_ge(slot_free, slot_number(i, t + 1, TURN_AT) + 1)
                    buf, c = t // QC % 2, t % QC
                    sp.dma_start(Q[ONE_ROW:ONE_ROW + 1, buf, c, :], shift[0:HG * ST, t % 2, :]).then_inc(shift_loaded[t % 2], 16)

                def store_heads(i, s):
                    sp.wait_ge(heads_ready, STEPS * i + (s + 1))
                    sp.dma_start(s_heads[bass.ds(i * (STEPS * P) + s * P, P), :], heads[:, s % 2, :]
                                 ).then_inc(heads_stored[s % 2], 16)

                def turn(i, last):
                    load_unit(i, 1)
                    load_shift(i, 1)
                    store_heads(i, 0)
                    load_shift(i, 2)
                    if not last:
                        load_unit(i, 2)
                    store_heads(i, 1)
                    load_shift(i, 3)
                    store_heads(i, 2)
                    if not last:
                        load_shift(i, 4)
                    store_heads(i, 3)

                sp.wait_ge(consts_ready, 4)
                load_unit(0, 0)
                for n, (src, _, _) in enumerate(pieces):
                    need = n - 1
                    if positive(need):
                        sp.wait_ge(w_lo_done, need)
                    to = w_stage[:, n % 2, :] if n < KT else w_stage[:, n % 2, :].rearrange("p (f d) -> p f d", f=RT)
                    sp.dma_start(to, src).then_inc(w_loaded[n % 2], 16)
                load_shift(0, 0)
                turns(sp, turn)
                for k in range(2):
                    sp.wait_ge(heads_stored[k], 16 * STEPS * TURNS // 2)

            @block.gpsimd
            def _(pool):
                def normalize(i, s):
                    S = STEPS * i + s
                    need = 16 * (STEPS // 2 * i + s // 2)
                    if positive(need):
                        pool.wait_ge(heads_stored[s % 2], need)
                    pool.wait_ge(o_copied, S + 1)
                    pool.wait_ge(rden_done, S + 1)
                    pool.tensor_tensor(heads[:, s % 2, :], o_raw[:, s % 2, :], rden[:, s % 2, :], ALU.mult
                                       ).then_inc(heads_ready, 1)

                def turn(i, last):
                    for t in range(PER):
                        G = PER * i + t
                        need = G - 1
                        if positive(need):
                            pool.wait_ge(den_done, need)
                        pool.wait_ge(exp_done, 4 * G + 4)
                        pool.tensor_tensor(pair_sum[:, t % 2], probs[:, t % 2, 0], probs[:, t % 2, 1], ALU.add
                                           ).then_inc(pair_sum_done, 1)
                        if t >= PAIRS and t % PAIRS == 1:
                            normalize(i, t // PAIRS - 1)
                    normalize(i, STEPS - 1)

                pool.memset(neg_max[:], 0.0).then_inc(consts_ready, 1)
                for n, (_, hi, lo) in enumerate(pieces):
                    pool.wait_ge(w_hi_done, n + 1)
                    pool.tensor_tensor(lo, w_stage[:, n % 2], hi, ALU.subtract).then_inc(w_lo_done, 1)
                turns(pool, turn)

            @block.scalar
            def _(act):
                def copy_o(i, s):
                    S = STEPS * i + s
                    act.wait_ge(pv_done, PER * i + PAIRS * (s + 1))
                    need = S - 1
                    if positive(need):
                        act.wait_ge(heads_ready, need)
                    act.activation(o_raw[:, s % 2, :], banks[:, 6, :], ACT.Copy).then_inc(o_copied, 1)

                def turn(i, last):
                    for t in range(PER):
                        G = PER * i + t
                        need = G - 1
                        if positive(need):
                            act.wait_ge(pv_done, need)
                        need = G - 1
                        if positive(need):
                            act.wait_ge(pair_sum_done, need)
                        for q in range(4):
                            act.wait_ge(scores_ready, 4 * G + (q + 1))
                            act.activation(probs[:, t % 2, q // 2, 2 * (q % 2):2 * (q % 2) + 2, :],
                                           banks[:, 2 * (q % 2):2 * (q % 2) + 2, :], ACT.Exp).then_inc(exp_done, 1)
                        if t >= PAIRS and t % PAIRS == 0:
                            copy_o(i, t // PAIRS - 1)
                    copy_o(i, STEPS - 1)

                for n, (_, hi, _) in enumerate(pieces):
                    act.wait_ge(w_loaded[n % 2], 16 * (n // 2 + 1))
                    act.activation(hi, w_stage[:, n % 2], ACT.Copy).then_inc(w_hi_done, 1)
                turns(act, turn)

            @block.vector
            def _(dve):
                def slot(i, t, k):
                    n = slot_number(i, t, k)
                    par = t % 2
                    dve.wait_ge(slot_filled, n + 1)
                    bank = banks[:, 4 + (SLOTS * t + k) % 2, :]
                    if k == TURN_AT:
                        need = 16 * (STEPS // 2 * i + (t - 1) // 2)
                        if positive(need):
                            dve.wait_ge(shift_loaded[1 - par], need)
                        dve.tensor_copy(shift[0:HG * ST, 1 - par, :], bank[0:HG * ST, 0:P]).then_inc(slot_free, 1)
                        return
                    item = k if k < TURN_AT else k - 1
                    dve.tensor_reduce(maxima[:, par, item:item + 1], bank, AX_X, ALU.max).then_inc(slot_free, 1)
                    if k == SLOTS - 1:
                        dve.wait_ge(slot_free, n + 1)
                        dve.tensor_reduce(neg_max[:, par, 0:HG * ST],
                                          maxima[:, par, :].rearrange("p (r c) -> p r c", c=CC), AX_X, ALU.max,
                                          negate=True).then_inc(neg_max_ready, 1)

                def invert(i, s):
                    S = STEPS * i + s
                    dve.wait_ge(den_done, PER * i + PAIRS * (s + 1))
                    need = S - 1
                    if positive(need):
                        dve.wait_ge(heads_ready, need)
                    dve.reciprocal(rden[:, s % 2, :], banks[:, 7, :]).then_inc(rden_done, 1)

                def turn(i, last):
                    for t in range(PER):
                        for when in slots_of(t // PAIRS, t % PAIRS, last):
                            slot(i, *when)
                        if t >= PAIRS and t % PAIRS == 1:
                            invert(i, t // PAIRS - 1)
                    invert(i, STEPS - 1)

                for tensor in (K, Q):
                    dve.memset(tensor[MASK_ROW:ROWS], 1.0).then_inc(consts_ready, 1)
                dve.memset(ones[:], 1.0).then_inc(consts_ready, 1)
                dve.wait_ge(consts_ready, 4)
                for when in OPENING:
                    slot(0, *when)
                turns(dve, turn)

            @block.tensor
            def _(pe):
                def slot(i, t, k):
                    n = slot_number(i, t, k)
                    need = n - 1
                    if positive(need):
                        pe.wait_ge(slot_free, need)
                    bank = banks[:, 4 + (SLOTS * t + k) % 2, :]
                    if k == TURN_AT:
                        need = STEPS * i + t
                        if positive(need):
                            pe.wait_ge(neg_max_ready, need)
                        pe.transpose(bank[:, 0:P], neg_max[:, 1 - t % 2, :], ident[:]).then_inc(slot_filled, 1)
                        return
                    buf, c = t // QC % 2, t % QC
                    if k == 0 and t % QC == 0:
                        pe.wait_ge(unit_loaded[buf], 16 * UNIT_DMAS * (i + t // (2 * QC) + 1))
                    h, tile, chunk = item_of(k)
                    pe.matmul(bank, Q[0:ONE_ROW, buf, c, h * N + tile * P:h * N + (tile + 1) * P],
                              K[0:ONE_ROW, buf, h, chunk * N:(chunk + 1) * N], start=True, stop=True
                              ).then_inc(slot_filled, 1)

                def scores(i, t, q):
                    s, j = t // PAIRS, 2 * (t % PAIRS) + q // 2
                    buf, c = s // QC, s % QC
                    if t % PAIRS == 0 and q == 0:
                        pe.wait_ge(shift_loaded[s % 2], 16 * (STEPS // 2 * i + (s // 2 + 1)))
                    need = 4 * (PER * i + t) + (q - 1)
                    if positive(need):
                        pe.wait_ge(exp_done, need)
                    for e in range(2):
                        h = 2 * (q % 2) + e
                        last = pe.matmul(banks[:, 2 * (q % 2) + e, :], K[0:ROWS, buf, h, j * P:(j + 1) * P],
                                         Q[0:ROWS, buf, c, h * N:(h + 1) * N], start=True, stop=True)
                    last.then_inc(scores_ready, 1)

                def values(i, t, jj):
                    s, p = t // PAIRS, t % PAIRS
                    if jj == 0:
                        pe.wait_ge(exp_done, 4 * (PER * i + t) + 4)
                        if p == 0:
                            need = STEPS * i + s
                            if positive(need):
                                pe.wait_ge(o_copied, need)
                    for h in range(HG):
                        last = pe.matmul(banks[h * W:(h + 1) * W, 6, :], V[:, s // QC, 2 * p + jj, h * W:(h + 1) * W],
                                         probs[:, t % 2, jj, h, :], start=(p == 0 and jj == 0),
                                         stop=(p == PAIRS - 1 and jj == 1))
                    if jj == 1:
                        last.then_inc(pv_done, 1)

                def denominators(i, t):
                    s, p = t // PAIRS, t % PAIRS
                    pe.wait_ge(pair_sum_done, PER * i + (t + 1))
                    if p == 0:
                        need = STEPS * i + s
                        if positive(need):
                            pe.wait_ge(rden_done, need)
                    for h in range(HG):
                        last = pe.matmul(banks[h * W:(h + 1) * W, 7, :], ones[:], pair_sum[:, t % 2, h, :],
                                         start=(p == 0), stop=(p == PAIRS - 1))
                    last.then_inc(den_done, 1)

                def turn(i, last):
                    for t in range(PER):
                        todo = slots_of(t // PAIRS, t % PAIRS, last)
                        for q in range(4):
                            scores(i, t, q)
                            for when in todo[q:q + 1]:
                                slot(i, *when)
                        if t >= 1:
                            values(i, t - 1, 0)
                        for when in todo[4:6]:
                            slot(i, *when)
                        if t >= 1:
                            values(i, t - 1, 1)
                        for when in todo[6:]:
                            slot(i, *when)
                        if t >= 2:
                            denominators(i, t - 2)
                    values(i, PER - 1, 0)
                    values(i, PER - 1, 1)
                    denominators(i, PER - 2)
                    denominators(i, PER - 1)

                pe.wait_ge(consts_ready, 4)
                for when in OPENING:
                    slot(0, *when)
                turns(pe, turn)


def ffn(nc, ident, banks, x, s_heads, g_attn, g_ffn, m1, m2, mb, b2, w1_h, w1_l, w2_h, w2_l, out):
    ITEMS = ST * (DFF // N)
    QT = DFF // N
    CHUNKS = 2
    PER = CHUNKS * ITEMS
    PREPS = ST + KT + 1
    GB = N // D2
    RT = N // P
    BIAS_HI, BIAS_LO = 0, W
    with ExitStack() as ctx:
        def sb(name, shape, dt):
            return ctx.enter_context(nc.sbuf_tensor(name, shape, dt))

        def sem(name):
            return ctx.enter_context(nc.semaphore(name))

        x_f = sb("c_x", [P, 2, ST, D], F32)
        heads = sb("c_heads", [P, 2, GROUPS, N], F32)
        x1 = sb("x1", [P, 2, ST, D], F32)
        xn = sb("c_xn", [P, ST, D], F32)
        xT_h = sb("c_xT_h", [P, 2, KT, N], F16)
        xT_l = sb("c_xT_l", [P, 2, KT, N], F16)
        lr_h = sb("lr_h", [P, 2, N], F16)
        lr_l = sb("lr_l", [P, 2, N], F16)
        peak = sb("peak", [P, 2, GB], F32)
        is_peak = sb("is_peak", [P, 2, N], F32)
        goes_on = sb("goes_on", [P, N], F32)
        count = sb("count", [P, 2, N], F32)
        relu = sb("relu", [P, 2, N], F32)
        act_f = sb("act_f", [P, 2, N], F32)
        aT_h = sb("aT_h", [P, 2, RT, P], F16)
        aT_l = sb("aT_l", [P, 2, RT, P], F16)
        y = sb("y", [P, 2, D], F32)
        result = sb("result", [P, 2, D], F32)
        gate = sb("gate", [P, 2, 2], F32)
        b2_f = sb("b2_f", [P, D], F32)
        m1_f = sb("m1_f", [P, KT, 2 * DL], F32)
        m1_h = sb("m1_h", [P, KT, 2 * DL], F16)
        m1_l = sb("m1_l", [P, KT, 2 * DL], F16)
        m2_f = sb("m2_f", [P, DFF], F32)
        mb_f = sb("mb_f", [2 * W, DFF], F32)
        mb_h = sb("mb_h", [2 * W, DFF], F16)
        m2_1 = sb("m2_1", [P, DFF], F16)
        m2_2 = sb("m2_2", [P, DFF], F16)
        stats = sb("c_stats", [P, ST, 6], F32)
        moments = sb("c_moments", [P, 3, ST], F32)
        small = sb("c_small", [P, 5, ST], F32)

        consts_loaded = sem("c_consts_loaded")
        zeros_ready = sem("zeros_ready")
        consts_hi = sem("c_consts_hi")
        consts_ready = sem("c_consts_ready")
        rows_loaded = [sem(f"rows_loaded{i}") for i in range(2)]
        prep_filled = sem("prep_filled")
        prep_hi = sem("prep_hi")
        prep_free = sem("prep_free")
        ln_step = sem("c_ln_step")
        sqrt_done = sem("c_sqrt_done")
        logits_filled = sem("logits_filled")
        mid_filled = sem("mid_filled")
        aT_filled = sem("aT_filled")
        w2_done = sem("w2_done")
        peak_done = sem("peak_done")
        is_peak_done = sem("is_peak_done")
        count_done = sem("count_done")
        relu_done = sem("relu_done")
        act_done = sem("act_done")
        aT_hi_done = sem("aT_hi_done")
        aT_lo_done = sem("aT_lo_done")
        y_done = sem("y_done")
        result_ready = sem("result_ready")
        result_stored = [sem(f"result_stored{i}") for i in range(2)]

        LOADS = 1 + GROUPS
        PREP_BANK, Y_BANK = 7, 6

        def prep_at(t):
            return {0: [0], 1: [1], 2: [2], 3: [3], 7: [4], 8: [5], 9: [6], 10: [7], 12: [8]}.get(t, [])

        NORM_AT = 4

        def turns(eng, body):
            body(0, False)
            with eng.Fori(1, B - 1) as i:
                body(i, False)
            body(B - 1, True)

        with nc.Block() as block:
            @block.sync
            def _(sp):
                def load_rows(i, c):
                    need = PREPS * (2 * i + (c - 2)) + ST
                    if positive(need):
                        sp.wait_ge(prep_free, need)
                    sp.dma_start(x_f[:, c % 2], x[bass.ds(i * SQ + c * N, N), :].rearrange("(s p) d -> p s d", p=P)
                                 ).then_inc(rows_loaded[c % 2], 16)
                    for g in range(GROUPS):
                        start = (c // 2 * GROUPS + g) * QC + c % 2
                        sp.dma_start(heads[:, c % 2, g, :], s_heads[bass.ds(i * (GROUPS * QC * P) + start * P, P), :]
                                     ).then_inc(rows_loaded[c % 2], 16)

                def store(i, c, s):
                    n = ST * c + s
                    sp.wait_ge(result_ready, 2 * ST * i + (n + 1))
                    sp.dma_start(out[bass.ds(i * SQ + n * P, P), :], result[:, n % 2, :]
                                 ).then_inc(result_stored[n % 2], 16)

                def turn(i, last):
                    for c in range(CHUNKS):
                        for s in range(ST):
                            store(i, c, s)
                            if s == 0 and not last:
                                load_rows(i, c + 2)

                sp.dma_start(m1_f[:, :, 0:DL], m1.rearrange("(k p) l -> p k l", p=P)).then_inc(consts_loaded, 16)
                sp.dma_start(m1_f[:, :, DL:2 * DL], m1.rearrange("(k p) l -> p k l", p=P)).then_inc(consts_loaded, 16)
                for at in (0, DL):
                    sp.dma_start(m2_f[at:at + DL, :], m2).then_inc(consts_loaded, 16)
                for at in (BIAS_HI, BIAS_LO):
                    sp.dma_start(mb_f[at:at + 1, :], mb).then_inc(consts_loaded, 16)
                sp.dma_start(b2_f[:], b2.partition_broadcast(P)).then_inc(consts_loaded, 16)
                for n, g in enumerate((g_attn, g_ffn)):
                    sp.dma_start(gate[:, 0, n:n + 1], g.partition_broadcast(P)).then_inc(consts_loaded, 16)
                load_rows(0, 0)
                load_rows(0, 1)
                turns(sp, turn)
                for k in range(2):
                    sp.wait_ge(result_stored[k], 16 * (SQ // P * B // 2))

            @block.gpsimd
            def _(pool):
                pool.memset(m2_2[0:DL, :], 0.0).then_inc(zeros_ready, 1)
                pool.memset(lr_l[:], 1.0).then_inc(zeros_ready, 1)
                pool.memset(goes_on[:], 1.0).then_inc(zeros_ready, 1)
                pool.wait_ge(zeros_ready, 3)
                pool.memset(goes_on[:].rearrange("p (g d) -> p g d", d=D2)[:, :, 0:1], 0.0).then_inc(zeros_ready, 1)

            @block.scalar
            def _(act):
                def prep(i, c, n):
                    C = 2 * i + c
                    bank = banks[:, PREP_BANK, :]
                    if n < ST:
                        return
                    act.wait_ge(prep_filled, PREPS * C + (n + 1))
                    to = xT_h[:, c % 2, n - ST, :] if n < ST + KT else lr_h[:, c % 2, :]
                    act.activation(to, bank, ACT.Copy).then_inc(prep_hi, 1)

                def item(i, u):
                    U = PER * i + u
                    if isinstance(U, int) and U < 0:
                        return
                    act.wait_ge(aT_filled, U + 1)
                    need = U - 1
                    if positive(need):
                        act.wait_ge(w2_done, need)
                    act.activation(aT_h[:, u % 2].rearrange("p f t -> p (f t)"), banks[:, 4 + u % 2, :], ACT.Copy
                                   ).then_inc(aT_hi_done, 1)

                def turn(i, last):
                    for u in range(PER):
                        item(i, u - 1)
                        c, t = divmod(u, ITEMS)
                        if last and c == 1:
                            continue
                        for n in prep_at(t):
                            prep(i, c + 1, n)
                        if t == NORM_AT:
                            scalar_layer_norm(act, 2 * i + (c + 1), small, sqrt_done, ln_step)

                act.wait_ge(consts_loaded, 16 * 9)
                act.activation(gate[:, 1, :], gate[:, 0, :], ACT.Tanh).then_inc(consts_hi, 1)
                act.activation(m1_h[:], m1_f[:], ACT.Copy).then_inc(consts_hi, 1)
                act.activation(m2_1[0:DL, :], m2_f[0:DL, :], ACT.Copy).then_inc(consts_hi, 1)
                act.activation(m2_2[DL:2 * DL, :], m2_f[DL:2 * DL, :], ACT.Copy).then_inc(consts_hi, 1)
                act.activation(mb_h[BIAS_LO:BIAS_LO + 1, :], mb_f[BIAS_LO:BIAS_LO + 1, :], ACT.Copy).then_inc(consts_hi, 1)
                act.wait_ge(zeros_ready, 4)
                act.activation(m2_2[BIAS_HI:BIAS_HI + 1, :], mb_f[BIAS_HI:BIAS_HI + 1, :], ACT.Copy).then_inc(consts_hi, 1)
                scalar_layer_norm(act, 0, small, sqrt_done, ln_step)
                for n in range(PREPS):
                    prep(0, 0, n)
                turns(act, turn)
                item(0, PER * B - 1)

            @block.vector
            def _(dve):
                def prep(i, c, n):
                    C = 2 * i + c
                    bank = banks[:, PREP_BANK, :]
                    if n < ST:
                        dve.wait_ge(rows_loaded[c % 2], 16 * LOADS * (i + (c // 2 + 1)))
                        dve.wait_ge(prep_filled, PREPS * C + (n + 1))
                        ins = dve.scalar_tensor_tensor(x1[:, c % 2, n, :], bank, gate[:, 1, 0:1], x_f[:, c % 2, n, :],
                                                       ALU.mult, ALU.add)
                    else:
                        dve.wait_ge(prep_hi, (KT + 1) * C + (n - ST + 1))
                        if n < ST + KT:
                            ins = dve.tensor_tensor(xT_l[:, c % 2, n - ST, :], bank, xT_h[:, c % 2, n - ST, :],
                                                    ALU.subtract)
                        else:
                            ins = dve.tensor_tensor(lr_l[DL:2 * DL, c % 2, :], bank[DL:2 * DL, :],
                                                    lr_h[DL:2 * DL, c % 2, :], ALU.subtract)
                    ins.then_inc(prep_free, 1)

                def norm(i, c):
                    dve.wait_ge(prep_free, PREPS * (2 * i + c) + ST)
                    vector_layer_norm(dve, 2 * i + c, x1[:, c % 2], xn, stats, moments, small, sqrt_done, ln_step)

                def lo_part(i, u):
                    U = PER * i + u
                    if isinstance(U, int) and U < 0:
                        return
                    dve.wait_ge(aT_hi_done, U + 1)
                    dve.tensor_tensor(aT_l[:, u % 2].rearrange("p f t -> p (f t)"), banks[:, 4 + u % 2, :],
                                      aT_h[:, u % 2].rearrange("p f t -> p (f t)"), ALU.subtract
                                      ).then_inc(aT_lo_done, 1)

                def finish(i, u):
                    U = PER * i + u
                    if (isinstance(U, int) and U < 0) or u % QT != QT - 1:
                        return
                    R = ST * 2 * i + u // QT
                    r = u // QT % (2 * ST)
                    dve.wait_ge(w2_done, U + 1)
                    dve.tensor_tensor(y[:, r % 2, :], banks[:, Y_BANK, :], b2_f[:], ALU.add).then_inc(y_done, 1)
                    dve.wait_ge(y_done, R + 1)
                    need = 16 * (ST * i + u // QT // 2)
                    if positive(need):
                        dve.wait_ge(result_stored[r % 2], need)
                    dve.scalar_tensor_tensor(result[:, r % 2, :], y[:, r % 2, :], gate[:, 1, 1:2],
                                             x1[:, r // ST, r % ST, :], ALU.mult, ALU.add).then_inc(result_ready, 1)

                def item(i, u):
                    U = PER * i + u
                    par = u % 2
                    logits = banks[:, par, :].rearrange("p (g d) -> p g d", d=D2)
                    dve.wait_ge(logits_filled, U + 1)
                    dve.tensor_reduce(peak[:, par, :], logits, AX_X, ALU.max).then_inc(peak_done, 1)
                    dve.wait_ge(peak_done, U + 1)
                    dve.tensor_tensor(is_peak[:, par, :].rearrange("p (g d) -> p g d", d=D2), logits,
                                      peak[:, par, :].unsqueeze(2).to_broadcast([P, GB, D2]), ALU.is_equal
                                      ).then_inc(is_peak_done, 1)
                    dve.wait_ge(is_peak_done, U + 1)
                    dve.tensor_tensor_scan(count[:, par, :], goes_on[:], is_peak[:, par, :], 0.0, ALU.mult, ALU.add
                                           ).then_inc(count_done, 1)
                    dve.wait_ge(mid_filled, U + 1)
                    dve.scalar_tensor_tensor(relu[:, par, :], banks[:, 2 + par, :], 0.0, is_peak[:, par, :],
                                             ALU.max, ALU.mult).then_inc(relu_done, 1)
                    lo_part(i, u - 1)
                    dve.wait_ge(count_done, U + 1)
                    dve.wait_ge(relu_done, U + 1)
                    need = U - 1
                    if positive(need):
                        dve.wait_ge(aT_filled, need)
                    dve.scalar_tensor_tensor(act_f[:, par, :], count[:, par, :], 1.0, relu[:, par, :],
                                             ALU.is_equal, ALU.mult).then_inc(act_done, 1)

                def turn(i, last):
                    for u in range(PER):
                        item(i, u)
                        finish(i, u - 3)
                        c, t = divmod(u, ITEMS)
                        if last and c == 1:
                            continue
                        for n in prep_at(t):
                            prep(i, c + 1, n)
                        if t == NORM_AT:
                            norm(i, c + 1)

                dve.wait_ge(consts_hi, 6)
                dve.tensor_tensor(m1_l[:], m1_f[:], m1_h[:], ALU.subtract).then_inc(consts_ready, 1)
                dve.tensor_tensor(m2_1[DL:2 * DL, :], m2_f[DL:2 * DL, :], m2_2[DL:2 * DL, :], ALU.subtract
                                  ).then_inc(consts_ready, 1)
                dve.tensor_tensor(m2_2[BIAS_LO:BIAS_LO + 1, :], mb_f[BIAS_LO:BIAS_LO + 1, :],
                                  mb_h[BIAS_LO:BIAS_LO + 1, :], ALU.subtract).then_inc(consts_ready, 1)
                dve.wait_ge(zeros_ready, 4)
                for n in range(ST):
                    prep(0, 0, n)
                norm(0, 0)
                for n in range(ST, PREPS):
                    prep(0, 0, n)
                turns(dve, turn)
                lo_part(0, PER * B - 1)
                for u in range(PER * B - 3, PER * B):
                    finish(0, u)

            @block.tensor
            def _(pe):
                def prep(i, c, n):
                    C = 2 * i + c
                    bank = banks[:, PREP_BANK, :]
                    need = PREPS * C + n
                    if positive(need):
                        pe.wait_ge(prep_free, need)
                    if n < ST:
                        if n == 0:
                            pe.wait_ge(rows_loaded[c % 2], 16 * LOADS * (i + (c // 2 + 1)))
                        for g in range(GROUPS):
                            last = pe.transpose(bank[:, g * P:(g + 1) * P], heads[:, c % 2, g, n * P:(n + 1) * P],
                                                ident[:])
                    elif n < ST + KT:
                        k = n - ST
                        if k == 0:
                            pe.wait_ge(ln_step, LN_STEPS * (C + 1))
                        for s in range(ST):
                            last = pe.transpose(bank[:, s * P:(s + 1) * P], xn[:, s, k * P:(k + 1) * P], ident[:])
                    else:
                        last = pair_product(pe, bank, lambda k: (m1_h[:, k, :], m1_l[:, k, :]),
                                            lambda k: (xT_h[:, c % 2, k, :], xT_l[:, c % 2, k, :]))
                    last.then_inc(prep_filled, 1)

                def item(i, u):
                    U = PER * i + u
                    c, t = divmod(u, ITEMS)
                    s, q = divmod(t, QT)
                    rows, cols = slice(s * P, (s + 1) * P), slice(q * N, (q + 1) * N)
                    if t == 0:
                        pe.wait_ge(prep_free, PREPS * (2 * i + (c + 1)))
                    need = U - 1
                    if positive(need):
                        pe.wait_ge(is_peak_done, need)
                    logits = banks[:, u % 2, :]
                    pe.matmul(logits, lr_h[:, c, rows], m2_1[:, cols], start=True, stop=False)
                    pe.matmul(logits, lr_l[:, c, rows], m2_2[:, cols], start=False, stop=True
                              ).then_inc(logits_filled, 1)
                    need = U - 1
                    if positive(need):
                        pe.wait_ge(relu_done, need)
                    pair_product(pe, banks[:, 2 + u % 2, :], lambda k: (xT_h[:, c, k, rows], xT_l[:, c, k, rows]),
                                 lambda k: (w1_h[:, k, cols], w1_l[:, k, cols])).then_inc(mid_filled, 1)

                def turn_back(i, u):
                    U = PER * i + u
                    if isinstance(U, int) and U < 0:
                        return
                    pe.wait_ge(act_done, U + 1)
                    need = U - 1
                    if positive(need):
                        pe.wait_ge(aT_lo_done, need)
                    for a in range(RT):
                        last = pe.transpose(banks[:, 4 + u % 2, a * P:(a + 1) * P],
                                            act_f[:, u % 2, a * P:(a + 1) * P], ident[:])
                    last.then_inc(aT_filled, 1)

                def second(i, u):
                    U = PER * i + u
                    if isinstance(U, int) and U < 0:
                        return
                    q = u % QT
                    pe.wait_ge(aT_lo_done, U + 1)
                    if q == 0:
                        need = 2 * ST * i + u // QT
                        if positive(need):
                            pe.wait_ge(y_done, need)
                    pair_product(pe, banks[:, Y_BANK, :], lambda a: (aT_h[:, u % 2, a, :], aT_l[:, u % 2, a, :]),
                                 lambda a: (w2_h[:, q * RT + a, :], w2_l[:, q * RT + a, :]), range(RT),
                                 start=(q == 0), stop=(q == QT - 1)).then_inc(w2_done, 1)

                def turn(i, last):
                    for u in range(PER):
                        item(i, u)
                        turn_back(i, u - 1)
                        second(i, u - 2)
                        c, t = divmod(u, ITEMS)
                        if last and c == 1:
                            continue
                        for n in prep_at(t):
                            prep(i, c + 1, n)

                pe.wait_ge(consts_ready, 3)
                for n in range(PREPS):
                    prep(0, 0, n)
                turns(pe, turn)
                turn_back(0, PER * B - 1)
                second(0, PER * B - 2)
                second(0, PER * B - 1)


def build(nc, x, ctxT, mask, g_attn, g_ffn, WqT, bq, WkT, bk, WvT, bv, m1, m2, mb, w1, w2, b2, out):
    s_K = [nc.dram_tensor(f"s_K{n}", (B * D, SKV), F16).ap() for n in "hl"]
    s_Q = [nc.dram_tensor(f"s_Q{n}", (B * D, SQ), F16).ap() for n in "hl"]
    s_V = nc.dram_tensor("s_V", (UNITS * SKV, P), F32).ap()
    s_mask = nc.dram_tensor("s_mask", (UNITS, SKV), F16).ap()
    s_heads = nc.dram_tensor("s_heads", (UNITS * QC * P, N), F32).ap()
    with ExitStack() as ctx:
        ident = ctx.enter_context(nc.sbuf_tensor("ident", [P, P], F32))
        banks = ctx.enter_context(nc.psum_tensor("banks", [P, BANKS, N], F32))
        project(nc, ident, banks, x, ctxT, mask, WqT, WkT, WvT, bq, bk, bv, s_K, s_Q, s_V, s_mask)
        w1_h, w1_l = (ctx.enter_context(nc.sbuf_tensor(f"w1_{n}", [P, KT, DFF], F16)) for n in "hl")
        w2_h, w2_l = (ctx.enter_context(nc.sbuf_tensor(f"w2_{n}", [P, FT, D], F16)) for n in "hl")
        attend(nc, ident, banks, s_K, s_Q, s_V, s_mask, s_heads, w1, w2, w1_h, w1_l, w2_h, w2_l)
        ffn(nc, ident, banks, x, s_heads, g_attn, g_ffn, m1, m2, mb, b2, w1_h, w1_l, w2_h, w2_l, out)


def kernel(x, ctx_1024, mask_BxS2_ik0, g_xattn, g_ffn, L0_xattn_Wq, L0_xattn_bq, L0_xattn_Wk, L0_xattn_bk,
           L0_xattn_Wv, L0_xattn_bv, L0_ffn_m1, L0_ffn_m2, L0_ffn_mb, L0_ffn_w1, L0_ffn_w2, L0_ffn_b2):
    import numpy as _np
    import concourse.bacc as _bacc
    from concourse import mybir as _mybir
    from concourse.bass_utils import run_bass_kernel_spmd as _run

    a = _np.asarray
    laid_out = {
        "x": a(x).reshape(B * SQ, D),
        "ctxT": a(ctx_1024).transpose(0, 2, 1).reshape(B * D, SKV),
        "mask": a(mask_BxS2_ik0).repeat(GROUPS, axis=0),
        "g_attn": a(g_xattn),
        "g_ffn": a(g_ffn),
        "WqT": a(L0_xattn_Wq).T,
        "bq": a(L0_xattn_bq).reshape(KT, P).T,
        "WkT": a(L0_xattn_Wk).T,
        "bk": a(L0_xattn_bk).reshape(KT, P).T,
        "WvT": a(L0_xattn_Wv).T,
        "bv": a(L0_xattn_bv),
        "m1": a(L0_ffn_m1),
        "m2": a(L0_ffn_m2).reshape(DL, DFF),
        "mb": a(L0_ffn_mb).reshape(1, DFF),
        "w1": a(L0_ffn_w1).reshape(D, DFF),
        "w2": a(L0_ffn_w2).transpose(1, 0, 2).reshape(DFF, D),
        "b2": a(L0_ffn_b2),
    }
    nc = _bacc.Bacc("TRN2", target_bir_lowering=False, num_devices=1)
    arrays, args = {}, []
    for name, value in laid_out.items():
        value = _np.ascontiguousarray(value)
        arrays[f"in_{name}"] = value
        args.append(nc.dram_tensor(f"in_{name}", value.shape, _mybir.dt.from_np(value.dtype), kind="ExternalInput").ap())
    out = nc.dram_tensor("out_x", (B * SQ, D), _mybir.dt.float32, kind="ExternalOutput").ap()
    build(nc, *args, out)
    r = _run(nc, [arrays], core_ids=[0])
    return r.results[0]["out_x"].reshape(B, SQ, D)
```

```python
from contextlib import ExitStack

import concourse.bass as bass
from concourse import mybir

F32 = mybir.dt.float32
F16 = mybir.dt.float16
I32 = mybir.dt.int32
ACT = mybir.ActivationFunctionType
ALU = mybir.AluOpType
AX_X = mybir.AxisListType.X

P = 128
B, SQ, SKV, D, H = 4, 1024, 2048, 512, 16
W = D // H
SCALE = float(W) ** -0.5
MASKED = 10000.0
EPS = 1e-5
D1, D2 = 32, 64
DFF = D1 * D2
DL = 64
KT = D // P
FT = DFF // P
N = 512
BANKS = 8
HG = P // W
GROUPS = H // HG
UNITS = B * GROUPS
QC = SQ // N
CC = SKV // N
JT = SKV // P
ST = N // P
LN_STEPS = 10


def positive(value):
    return not isinstance(value, int) or value > 0


def vector_layer_norm(dve, n, rows, out, stats, moments, small, sqrt_done, step):
    base = LN_STEPS * n
    var_eps, root, inv, tmp, rstd = (small[:, k, :] for k in range(5))
    total, gap, mean = (moments[:, k, :] for k in range(3))
    for s in range(ST):
        last = dve.bn_stats(stats[:, s, :], rows[:, s, :])
    last.then_inc(step, 1)
    dve.wait_ge(step, base + 1)
    dve.tensor_tensor(total, stats[:, :, 1], stats[:, :, 4], ALU.add)
    dve.tensor_tensor(gap, stats[:, :, 1], stats[:, :, 4], ALU.subtract)
    dve.tensor_tensor(tmp, stats[:, :, 2], stats[:, :, 5], ALU.add).then_inc(step, 1)
    dve.wait_ge(step, base + 2)
    dve.tensor_scalar(mean, total, 0.5, None, ALU.mult)
    dve.tensor_tensor(inv, gap, gap, ALU.mult)
    dve.tensor_scalar(rstd, tmp, 1.0 / D, EPS, ALU.mult, ALU.add).then_inc(step, 1)
    dve.wait_ge(step, base + 3)
    dve.scalar_tensor_tensor(var_eps, inv, 0.25, rstd, ALU.mult, ALU.add).then_inc(step, 1)
    dve.wait_ge(sqrt_done, n + 1)
    dve.reciprocal(inv, root).then_inc(step, 1)
    dve.wait_ge(step, base + 5)
    dve.tensor_tensor(tmp, inv, inv, ALU.mult).then_inc(step, 1)
    dve.wait_ge(step, base + 6)
    dve.tensor_tensor(rstd, tmp, var_eps, ALU.mult).then_inc(step, 1)
    dve.wait_ge(step, base + 7)
    dve.tensor_scalar(tmp, rstd, -0.5, 1.5, ALU.mult, ALU.add).then_inc(step, 1)
    dve.wait_ge(step, base + 8)
    dve.tensor_tensor(rstd, inv, tmp, ALU.mult).then_inc(step, 1)
    dve.wait_ge(step, base + 9)
    for s in range(ST):
        last = dve.tensor_scalar(out[:, s, :], rows[:, s, :], mean[:, s:s + 1], rstd[:, s:s + 1],
                                 ALU.subtract, ALU.mult)
    last.then_inc(step, 1)


def scalar_layer_norm(act, n, small, sqrt_done, step):
    act.wait_ge(step, LN_STEPS * n + 4)
    act.activation(small[:, 1, :], small[:, 0, :], ACT.Sqrt).then_inc(sqrt_done, 1)


def pair_product(pe, out, left, right, tiles=range(KT), start=True, stop=True):
    for k in tiles:
        (lh, ll), (rh, rl) = left(k), right(k)
        pe.matmul(out, lh, rh, start=start and k == tiles[0], stop=False)
        pe.matmul(out, lh, rl, start=False, stop=False)
        last = pe.matmul(out, ll, rh, start=False, stop=stop and k == tiles[-1])
    return last


def project(nc, ident, banks, x, ctxT, mask, WqT, WkT, WvT, bq, bk, bv, s_K, s_Q, s_V, s_mask):
    with ExitStack() as ctx:
        def sb(name, shape, dt):
            return ctx.enter_context(nc.sbuf_tensor(name, shape, dt))

        def sem(name):
            return ctx.enter_context(nc.semaphore(name))

        w_f = [sb(f"w{n}_f", [P, KT, D], F32) for n in "qkv"]
        w_h = [sb(f"w{n}_h", [P, KT, D], F16) for n in "qkv"]
        w_l = [sb(f"w{n}_l", [P, KT, D], F16) for n in "qkv"]
        bq_f = sb("bq_f", [P, KT], F32)
        bq_s = sb("bq_s", [P, KT], F32)
        bk_f = sb("bk_f", [P, KT], F32)
        bv_f = sb("bv_f", [P, D], F32)
        mask_i = sb("mask_i", [UNITS, SKV], I32)
        mask_h = sb("mask_h", [UNITS, SKV], F16)
        ctx_f = sb("ctx_f", [P, 2, KT, N], F32)
        ctx_h = sb("ctx_h", [P, 2, KT, N], F16)
        ctx_l = sb("ctx_l", [P, 2, KT, N], F16)
        k_h = sb("k_h", [P, 2, KT, N], F16)
        k_l = sb("k_l", [P, 2, KT, N], F16)
        v_f = sb("v_f", [P, 2, ST, D], F32)
        x_f = sb("x_f", [P, QC, ST, D], F32)
        xn = sb("xn", [P, ST, D], F32)
        xT_h = sb("xT_h", [P, KT, N], F16)
        xT_l = sb("xT_l", [P, KT, N], F16)
        q_h = sb("q_h", [P, QC, KT, N], F16)
        q_l = sb("q_l", [P, QC, KT, N], F16)
        stats = sb("stats", [P, ST, 6], F32)
        moments = sb("moments", [P, 3, ST], F32)
        small = sb("small", [P, 5, ST], F32)

        weights_loaded = sem("weights_loaded")
        consts_loaded = sem("consts_loaded")
        wq_scaled = sem("wq_scaled")
        weights_hi = sem("weights_hi")
        weights_ready = sem("weights_ready")
        mask_ready = sem("mask_ready")
        mask_stored = sem("mask_stored")
        ctx_loaded = [sem(f"ctx_loaded{i}") for i in range(2)]
        ctx_hi_done = sem("ctx_hi_done")
        ctx_lo_done = sem("ctx_lo_done")
        x_loaded = [sem(f"x_loaded{i}") for i in range(QC)]
        ln_step = sem("ln_step")
        sqrt_done = sem("sqrt_done")
        bank_filled = sem("bank_filled")
        hi_done = sem("hi_done")
        bank_free = sem("bank_free")
        kv_stored = [sem(f"kv_stored{i}") for i in range(2)]
        q_stored = [sem(f"q_stored{i}") for i in range(QC)]
        ident_zero = sem("ident_zero")
        ident_ready = sem("ident_ready")

        JOBS = [("KV", 0), ("T", 0), ("KV", 1), ("Q", 0), ("T", 1), ("KV", 2), ("Q", 1), ("KV", 3)]
        SIZE = {"KV": KT + ST, "T": KT, "Q": KT}
        HIS = KT
        first, at = {}, 0
        for job in JOBS:
            first[job] = at
            at += SIZE[job[0]]
        PER = at
        assert PER % BANKS == 0
        KV_DMAS = 2 + GROUPS

        def through(b, job):
            return PER * b + (first[job] + SIZE[job[0]])

        def before_T(b, c):
            return through(b, ("Q", 0)) if c else through(b - 1, ("Q", 1))

        with nc.Block() as block:
            @block.sync
            def _(sp):
                for f, w in zip(w_f, (WqT, WkT, WvT)):
                    sp.dma_start(f[:], w.rearrange("(k p) o -> p k o", p=P)).then_inc(weights_loaded, 16)
                sp.dma_start(bq_f[:], bq).then_inc(consts_loaded, 16)
                sp.dma_start(bk_f[:], bk).then_inc(consts_loaded, 16)
                sp.dma_start(bv_f[:], bv.partition_broadcast(P)).then_inc(consts_loaded, 16)
                sp.dma_start(mask_i[:], mask).then_inc(consts_loaded, 16)
                sp.wait_ge(mask_ready, 1)
                sp.dma_start(s_mask, mask_h[:]).then_inc(mask_stored, 16)

                def batch(b):
                    for kind, c in JOBS:
                        if kind == "KV":
                            sp.wait_ge(bank_free, through(b, (kind, c)))
                            for s_k, k in zip(s_K, (k_h, k_l)):
                                sp.dma_start(
                                    s_k[bass.ds(b * D, D), c * N:(c + 1) * N].rearrange("(m p) t -> p m t", p=P),
                                    k[:, c % 2]).then_inc(kv_stored[c % 2], 16)
                            for g in range(GROUPS):
                                sp.dma_start(
                                    s_V[bass.ds(b * (GROUPS * SKV) + (g * SKV + c * N), N), :].rearrange(
                                        "(s p) e -> p s e", p=P),
                                    v_f[:, c % 2, :, g * P:(g + 1) * P]).then_inc(kv_stored[c % 2], 16)
                        if kind == "Q":
                            sp.wait_ge(bank_free, through(b, (kind, c)))
                            for s_q, q in zip(s_Q, (q_h, q_l)):
                                sp.dma_start(
                                    s_q[bass.ds(b * D, D), c * N:(c + 1) * N].rearrange("(m p) t -> p m t", p=P),
                                    q[:, c]).then_inc(q_stored[c], 16)

                batch(0)
                with sp.Fori(1, B) as b:
                    batch(b)
                sp.wait_ge(mask_stored, 16)
                for i in range(2):
                    sp.wait_ge(kv_stored[i], 16 * KV_DMAS * B * CC // 2)
                    sp.wait_ge(q_stored[i], 16 * 2 * B)

            @block.gpsimd
            def _(pool):
                def load_ctx(b, c):
                    need = CC * b + (c - 1)
                    if positive(need):
                        pool.wait_ge(ctx_lo_done, need)
                    pool.dma_start(ctx_f[:, c % 2],
                                   ctxT[bass.ds(b * D, D), c * N:(c + 1) * N].rearrange("(k p) t -> p k t", p=P)
                                   ).then_inc(ctx_loaded[c % 2], 16)

                def load_x(b, c):
                    need = LN_STEPS * (QC * b + (c - 1))
                    if positive(need):
                        pool.wait_ge(ln_step, need)
                    pool.dma_start(x_f[:, c], x[bass.ds(b * SQ + c * N, N), :].rearrange("(s p) d -> p s d", p=P)
                                   ).then_inc(x_loaded[c], 16)

                def batch(b):
                    load_ctx(b, 0)
                    load_x(b, 0)
                    load_ctx(b, 1)
                    load_x(b, 1)
                    for c in range(CC):
                        pool.wait_ge(ctx_hi_done, CC * b + (c + 1))
                        pool.tensor_tensor(ctx_l[:, c % 2], ctx_f[:, c % 2], ctx_h[:, c % 2], ALU.subtract
                                           ).then_inc(ctx_lo_done, 1)
                        if c + 2 < CC:
                            load_ctx(b, c + 2)

                pool.memset(ident[:], 0.0).then_inc(ident_zero, 1)
                pool.wait_ge(ident_zero, 1)
                pool.affine_select(out=ident[:], in_=ident[:], compare_op=ALU.not_equal, fill=1.0, base=0,
                                   pattern=[[-1, P]], channel_multiplier=1).then_inc(ident_ready, 1)
                batch(0)
                with pool.Fori(1, B) as b:
                    batch(b)

            @block.scalar
            def _(act):
                def ctx_hi(b, c):
                    act.wait_ge(ctx_loaded[c % 2], 32 * b + 16 * (c // 2 + 1))
                    need = through(b, ("KV", c - 2)) if c >= 2 else through(b - 1, ("KV", c + 2))
                    if positive(need):
                        act.wait_ge(bank_filled, need)
                    act.activation(ctx_h[:, c % 2], ctx_f[:, c % 2], ACT.Copy).then_inc(ctx_hi_done, 1)

                def batch(b):
                    ctx_hi(b, 0)
                    scalar_layer_norm(act, QC * b, small, sqrt_done, ln_step)
                    ctx_hi(b, 1)
                    for kind, c in JOBS:
                        for g in range(HIS):
                            if g == 0 and kind == "KV":
                                need = 16 * KV_DMAS * (2 * b + c // 2)
                                if positive(need):
                                    act.wait_ge(kv_stored[c % 2], need)
                            if g == 0 and kind == "Q":
                                need = 32 * b
                                if positive(need):
                                    act.wait_ge(q_stored[c], need)
                            if g == 0 and kind == "T":
                                need = before_T(b, c)
                                if positive(need):
                                    act.wait_ge(bank_filled, need)
                            n = first[(kind, c)] + g
                            src = banks[:, n % BANKS, :]
                            act.wait_ge(bank_filled, PER * b + (n + 1))
                            if kind == "KV":
                                ins = act.activation(k_h[:, c % 2, g, :], src, ACT.Identity, bias=bk_f[:, g:g + 1])
                            elif kind == "Q":
                                ins = act.activation(q_h[:, c, g, :], src, ACT.Identity, bias=bq_s[:, g:g + 1])
                            else:
                                ins = act.activation(xT_h[:, g, :], src, ACT.Copy)
                            ins.then_inc(hi_done, 1)
                        if (kind, c) == ("T", 0):
                            scalar_layer_norm(act, QC * b + 1, small, sqrt_done, ln_step)
                        if kind == "KV" and c < 2:
                            ctx_hi(b, c + 2)

                for n in range(3):
                    if n == 0:
                        act.wait_ge(wq_scaled, 2)
                    else:
                        act.wait_ge(weights_loaded, 48)
                    act.activation(w_h[n][:], w_f[n][:], ACT.Copy).then_inc(weights_hi, 1)
                act.wait_ge(consts_loaded, 64)
                batch(0)
                with act.Fori(1, B) as b:
                    batch(b)

            @block.vector
            def _(dve):
                def norm(b, c):
                    dve.wait_ge(x_loaded[c], 16 * b + 16)
                    need = through(b, ("T", 0)) if c else through(b - 1, ("T", 1))
                    if positive(need):
                        dve.wait_ge(bank_filled, need)
                    vector_layer_norm(dve, QC * b + c, x_f[:, c], xn, stats, moments, small, sqrt_done, ln_step)

                def batch(b):
                    norm(b, 0)
                    for j, (kind, c) in enumerate(JOBS):
                        for g in range(SIZE[kind]):
                            n = first[(kind, c)] + g
                            src = banks[:, n % BANKS, :]
                            if g < HIS:
                                dve.wait_ge(hi_done, HIS * len(JOBS) * b + (HIS * j + g + 1))
                            else:
                                if g == HIS:
                                    need = 16 * KV_DMAS * (2 * b + c // 2)
                                    if positive(need):
                                        dve.wait_ge(kv_stored[c % 2], need)
                                dve.wait_ge(bank_filled, PER * b + (n + 1))
                            if kind == "KV" and g < HIS:
                                ins = dve.scalar_tensor_tensor(k_l[:, c % 2, g, :], src, bk_f[:, g:g + 1],
                                                               k_h[:, c % 2, g, :], ALU.add, ALU.subtract)
                            elif kind == "KV":
                                ins = dve.tensor_tensor(v_f[:, c % 2, g - HIS, :], src, bv_f[:], ALU.add)
                            elif kind == "Q":
                                ins = dve.scalar_tensor_tensor(q_l[:, c, g, :], src, bq_s[:, g:g + 1],
                                                               q_h[:, c, g, :], ALU.add, ALU.subtract)
                            else:
                                ins = dve.tensor_tensor(xT_l[:, g, :], src, xT_h[:, g, :], ALU.subtract)
                            ins.then_inc(bank_free, 1)
                        if (kind, c) == ("T", 0):
                            norm(b, 1)

                dve.wait_ge(weights_loaded, 48)
                dve.tensor_scalar(w_f[0][:], w_f[0][:], SCALE, None, ALU.mult).then_inc(wq_scaled, 1)
                dve.wait_ge(consts_loaded, 64)
                dve.tensor_scalar(bq_s[:], bq_f[:], SCALE, None, ALU.mult).then_inc(wq_scaled, 1)
                dve.tensor_scalar(mask_h[:], mask_i[:], MASKED, -MASKED, ALU.mult, ALU.add).then_inc(mask_ready, 1)
                for n in range(3):
                    dve.wait_ge(weights_hi, n + 1)
                    dve.tensor_tensor(w_l[n][:], w_f[n][:], w_h[n][:], ALU.subtract).then_inc(weights_ready, 1)
                dve.wait_ge(wq_scaled, 2)
                batch(0)
                with dve.Fori(1, B) as b:
                    batch(b)

            @block.tensor
            def _(pe):
                def weight(n, cols):
                    return lambda k: (w_h[n][:, k, cols], w_l[n][:, k, cols])

                def batch(b):
                    for kind, c in JOBS:
                        if kind == "KV":
                            pe.wait_ge(ctx_lo_done, CC * b + (c + 1))
                        elif kind == "T":
                            pe.wait_ge(ln_step, LN_STEPS * (QC * b + (c + 1)))
                        else:
                            pe.wait_ge(bank_free, through(b, ("T", c)))
                        for g in range(SIZE[kind]):
                            n = first[(kind, c)] + g
                            bank = banks[:, n % BANKS, :]
                            need = PER * b + (n + 1 - BANKS)
                            if positive(need):
                                pe.wait_ge(bank_free, need)
                            if kind == "KV" and g < HIS:
                                last = pair_product(pe, bank, weight(1, slice(g * P, (g + 1) * P)),
                                                    lambda k: (ctx_h[:, c % 2, k, :], ctx_l[:, c % 2, k, :]))
                            elif kind == "KV":
                                rows = slice((g - HIS) * P, (g - HIS + 1) * P)
                                last = pair_product(pe, bank,
                                                    lambda k: (ctx_h[:, c % 2, k, rows], ctx_l[:, c % 2, k, rows]),
                                                    weight(2, slice(0, D)))
                            elif kind == "Q":
                                last = pair_product(pe, bank, weight(0, slice(g * P, (g + 1) * P)),
                                                    lambda k: (xT_h[:, k, :], xT_l[:, k, :]))
                            else:
                                for s in range(ST):
                                    last = pe.transpose(bank[:, s * P:(s + 1) * P], xn[:, s, g * P:(g + 1) * P],
                                                        ident[:])
                            last.then_inc(bank_filled, 1)

                pe.wait_ge(weights_ready, 3)
                pe.wait_ge(ident_ready, 1)
                batch(0)
                with pe.Fori(1, B) as b:
                    batch(b)


def attend(nc, ident, banks, s_K, s_Q, s_V, s_mask, s_heads, s_den, w1, w2, w1_h, w1_l, w2_h, w2_l):
    HI0, HI1, LO, MASK_ROW, ONE_ROW, ROWS = 0, W, 2 * W, 3 * W, 3 * W + 1, 3 * W + 2
    STEPS = 2 * QC
    TURNS = UNITS // 2
    PAIRS = JT // 2
    PER = STEPS * PAIRS
    ITEMS = HG * ST * CC
    SLOTS = ITEMS + 1
    TURN_AT = 2
    AHEAD = 2 * PAIRS
    UNIT_DMAS = 3 + 3 * QC + HG + 2
    with ExitStack() as ctx:
        def sb(name, shape, dt):
            return ctx.enter_context(nc.sbuf_tensor(name, shape, dt))

        def sem(name):
            return ctx.enter_context(nc.semaphore(name))

        K = sb("K_stack", [ROWS, 2, HG, SKV], F16)
        Q = sb("Q_stack", [ROWS, 2, QC, HG * N], F16)
        V = sb("V", [P, 2, JT, P], F32)
        probs = sb("probs", [P, 2, 2, HG, N], F32)
        pair_sum = sb("pair_sum", [P, 2, HG, N], F32)
        ones = sb("ones", [P, W], F32)
        maxima = sb("maxima", [P, 2, ITEMS], F32)
        neg_max = sb("neg_max", [P, 2, P], F32)
        shift = sb("shift", [P, 2, P], F16)
        o_raw = sb("o_raw", [P, 2, N], F32)
        den = sb("den", [P, 2, N], F32)
        w_stage = sb("w_stage", [P, 2, DFF], F32)

        consts_ready = sem("b_consts_ready")
        unit_loaded = [sem(f"unit_loaded{i}") for i in range(2)]
        slot_filled = sem("slot_filled")
        slot_free = sem("slot_free")
        neg_max_ready = sem("neg_max_ready")
        shift_loaded = [sem(f"shift_loaded{i}") for i in range(2)]
        scores_ready = sem("scores_ready")
        exp_done = sem("exp_done")
        pv_done = sem("pv_done")
        pair_sum_done = sem("pair_sum_done")
        den_done = sem("den_done")
        o_copied = sem("o_copied")
        den_copied = sem("den_copied")
        heads_stored = [sem(f"heads_stored{i}") for i in range(2)]
        w_loaded = [sem(f"w_loaded{i}") for i in range(2)]
        w_hi_done = sem("w_hi_done")
        w_lo_done = sem("w_lo_done")

        RT = DFF // D
        pieces = [(w1[k * P:(k + 1) * P, :], w1_h[:, k, :], w1_l[:, k, :]) for k in range(KT)]
        pieces += [(w2[k * RT * P:(k + 1) * RT * P, :].rearrange("(f p) d -> p f d", p=P),
                    w2_h[:, RT * k:RT * (k + 1), :].rearrange("p f d -> p (f d)"),
                    w2_l[:, RT * k:RT * (k + 1), :].rearrange("p f d -> p (f d)")) for k in range(FT // RT)]

        def slot_runs(s, p):
            start = SLOTS * (s + 1) + AHEAD + 8 * p + (p > 0)
            return [divmod(n, SLOTS) for n in range(start, start + 8 + (p == 0))]

        def slots_of(s, p, last):
            return [(t, k) for t, k in slot_runs(s, p) if not last or t < STEPS or (t == STEPS and k == TURN_AT)]

        def item_of(k):
            item = k if k < TURN_AT else k - 1
            return item // (ST * CC), item // CC % ST, item % CC

        def first(i):
            return isinstance(i, int) and i == 0

        def turns(eng, body):
            body(0, False)
            with eng.Fori(1, TURNS - 1) as i:
                body(i, False)
            body(TURNS - 1, True)

        OPENING = [(0, k) for k in range(SLOTS)] + [(1, k) for k in range(AHEAD)]

        def slot_number(i, t, k):
            skipped = TURN_AT if isinstance(i, int) and i == TURNS - 1 and t == STEPS else 0
            return SLOTS * STEPS * i + (SLOTS * t + k - skipped)

        with nc.Block() as block:
            @block.sync
            def _(sp):
                def load_unit(i, u):
                    need = PER * i + (u - 1) * (PER // 2)
                    if positive(need):
                        sp.wait_ge(pv_done, need)
                    buf, got = u % 2, unit_loaded[u % 2]
                    rows = bass.ds(i * (2 * P) + u * P, P)
                    for at, s_k in ((HI0, s_K[0]), (HI1, s_K[0]), (LO, s_K[1])):
                        sp.dma_start(K[at:at + W, buf], s_k[rows, :].rearrange("(h w) t -> w h t", w=W)).then_inc(got, 16)
                    for at, s_q in ((HI0, s_Q[0]), (HI1, s_Q[1]), (LO, s_Q[0])):
                        for c in range(QC):
                            sp.dma_start(Q[at:at + W, buf, c, :].rearrange("w (h t) -> w h t", h=HG),
                                         s_q[rows, c * N:(c + 1) * N].rearrange("(h w) t -> w h t", w=W)
                                         ).then_inc(got, 16)
                    for h in range(HG):
                        sp.dma_start(K[MASK_ROW:MASK_ROW + 1, buf, h, :], s_mask[bass.ds(i * 2 + u, 1), :]
                                     ).then_inc(got, 16)
                    half = SKV // 2
                    for k in range(2):
                        sp.dma_start(V[:, buf, k * JT // 2:(k + 1) * JT // 2, :],
                                     s_V[bass.ds(i * (2 * SKV) + (u * SKV + k * half), half), :].rearrange(
                                         "(j p) e -> p j e", p=P)).then_inc(got, 16)

                def load_shift(i, t):
                    sp.wait_ge(slot_free, slot_number(i, t + 1, TURN_AT) + 1)
                    buf, c = t // QC % 2, t % QC
                    sp.dma_start(Q[ONE_ROW:ONE_ROW + 1, buf, c, :], shift[0:HG * ST, t % 2, :]).then_inc(shift_loaded[t % 2], 16)

                def store_heads(i, s):
                    sp.wait_ge(o_copied, STEPS * i + (s + 1))
                    sp.dma_start(s_heads[bass.ds(i * (STEPS * P) + s * P, P), :], o_raw[:, s % 2, :]
                                 ).then_inc(heads_stored[s % 2], 16)
                    sp.wait_ge(den_copied, STEPS * i + (s + 1))
                    sp.dma_start(s_den[bass.ds(i * (STEPS * HG) + s * HG, HG), :], den[0:P:W, s % 2, :]
                                 ).then_inc(heads_stored[s % 2], 16)

                def turn(i, last):
                    load_unit(i, 1)
                    if not first(i):
                        store_heads(i, -1)
                    load_shift(i, 1)
                    store_heads(i, 0)
                    load_shift(i, 2)
                    if not last:
                        load_unit(i, 2)
                    store_heads(i, 1)
                    load_shift(i, 3)
                    store_heads(i, 2)
                    if not last:
                        load_shift(i, 4)

                sp.wait_ge(consts_ready, 4)
                load_unit(0, 0)
                for n, (src, _, _) in enumerate(pieces):
                    need = n - 1
                    if positive(need):
                        sp.wait_ge(w_lo_done, need)
                    to = w_stage[:, n % 2, :] if n < KT else w_stage[:, n % 2, :].rearrange("p (f d) -> p f d", f=RT)
                    sp.dma_start(to, src).then_inc(w_loaded[n % 2], 16)
                load_shift(0, 0)
                turns(sp, turn)
                store_heads(TURNS - 1, STEPS - 1)
                for k in range(2):
                    sp.wait_ge(heads_stored[k], 32 * STEPS * TURNS // 2)

            @block.gpsimd
            def _(pool):
                def turn(i, last):
                    for t in range(PER):
                        G = PER * i + t
                        need = G - 1
                        if positive(need):
                            pool.wait_ge(den_done, need)
                        pool.wait_ge(exp_done, 4 * G + 4)
                        pool.tensor_tensor(pair_sum[:, t % 2], probs[:, t % 2, 0], probs[:, t % 2, 1], ALU.add
                                           ).then_inc(pair_sum_done, 1)

                pool.memset(neg_max[:], 0.0).then_inc(consts_ready, 1)
                for n, (_, hi, lo) in enumerate(pieces):
                    pool.wait_ge(w_hi_done, n + 1)
                    pool.tensor_tensor(lo, w_stage[:, n % 2], hi, ALU.subtract).then_inc(w_lo_done, 1)
                turns(pool, turn)

            @block.scalar
            def _(act):
                def copy_out(i, s, done, value, bank, to, copied):
                    act.wait_ge(done, value)
                    need = 32 * (STEPS // 2 * i + s // 2)
                    if positive(need):
                        act.wait_ge(heads_stored[s % 2], need)
                    act.activation(to[:, s % 2, :], banks[:, bank, :], ACT.Copy).then_inc(copied, 1)

                def copy_o(i, s):
                    copy_out(i, s, pv_done, PER * i + PAIRS * (s + 1), 6, o_raw, o_copied)

                def copy_den(i, s):
                    copy_out(i, s, den_done, PER * i + PAIRS * (s + 1), 7, den, den_copied)

                def turn(i, last):
                    for t in range(PER):
                        G = PER * i + t
                        need = G - 1
                        if positive(need):
                            act.wait_ge(pv_done, need)
                        need = G - 1
                        if positive(need):
                            act.wait_ge(pair_sum_done, need)
                        for q in range(4):
                            act.wait_ge(scores_ready, 4 * G + (q + 1))
                            act.activation(probs[:, t % 2, q // 2, 2 * (q % 2):2 * (q % 2) + 2, :],
                                           banks[:, 2 * (q % 2):2 * (q % 2) + 2, :], ACT.Exp).then_inc(exp_done, 1)
                        if t % PAIRS == 0 and not (first(i) and t < PAIRS):
                            copy_o(i, t // PAIRS - 1)
                        if t % PAIRS == 1 and not (first(i) and t < PAIRS):
                            copy_den(i, t // PAIRS - 1)

                for n, (_, hi, _) in enumerate(pieces):
                    act.wait_ge(w_loaded[n % 2], 16 * (n // 2 + 1))
                    act.activation(hi, w_stage[:, n % 2], ACT.Copy).then_inc(w_hi_done, 1)
                turns(act, turn)
                copy_o(TURNS - 1, STEPS - 1)
                copy_den(TURNS - 1, STEPS - 1)

            @block.vector
            def _(dve):
                def slot(i, t, k):
                    n = slot_number(i, t, k)
                    par = t % 2
                    dve.wait_ge(slot_filled, n + 1)
                    bank = banks[:, 4 + (SLOTS * t + k) % 2, :]
                    if k == TURN_AT:
                        need = 16 * (STEPS // 2 * i + (t - 1) // 2)
                        if positive(need):
                            dve.wait_ge(shift_loaded[1 - par], need)
                        dve.tensor_copy(shift[0:HG * ST, 1 - par, :], bank[0:HG * ST, 0:P]).then_inc(slot_free, 1)
                        return
                    item = k if k < TURN_AT else k - 1
                    dve.tensor_reduce(maxima[:, par, item:item + 1], bank, AX_X, ALU.max).then_inc(slot_free, 1)
                    if k == SLOTS - 1:
                        dve.wait_ge(slot_free, n + 1)
                        dve.tensor_reduce(neg_max[:, par, 0:HG * ST],
                                          maxima[:, par, :].rearrange("p (r c) -> p r c", c=CC), AX_X, ALU.max,
                                          negate=True).then_inc(neg_max_ready, 1)

                def turn(i, last):
                    for t in range(PER):
                        for when in slots_of(t // PAIRS, t % PAIRS, last):
                            slot(i, *when)

                for tensor in (K, Q):
                    dve.memset(tensor[MASK_ROW:ROWS], 1.0).then_inc(consts_ready, 1)
                dve.memset(ones[:], 1.0).then_inc(consts_ready, 1)
                dve.wait_ge(consts_ready, 4)
                for when in OPENING:
                    slot(0, *when)
                turns(dve, turn)

            @block.tensor
            def _(pe):
                def slot(i, t, k):
                    n = slot_number(i, t, k)
                    need = n - 1
                    if positive(need):
                        pe.wait_ge(slot_free, need)
                    bank = banks[:, 4 + (SLOTS * t + k) % 2, :]
                    if k == TURN_AT:
                        need = STEPS * i + t
                        if positive(need):
                            pe.wait_ge(neg_max_ready, need)
                        pe.transpose(bank[:, 0:P], neg_max[:, 1 - t % 2, :], ident[:]).then_inc(slot_filled, 1)
                        return
                    buf, c = t // QC % 2, t % QC
                    if k == 0 and t % QC == 0:
                        pe.wait_ge(unit_loaded[buf], 16 * UNIT_DMAS * (i + t // (2 * QC) + 1))
                    h, tile, chunk = item_of(k)
                    pe.matmul(bank, Q[0:ONE_ROW, buf, c, h * N + tile * P:h * N + (tile + 1) * P],
                              K[0:ONE_ROW, buf, h, chunk * N:(chunk + 1) * N], start=True, stop=True
                              ).then_inc(slot_filled, 1)

                def scores(i, t, q):
                    s, j = t // PAIRS, 2 * (t % PAIRS) + q // 2
                    buf, c = s // QC, s % QC
                    if t % PAIRS == 0 and q == 0:
                        pe.wait_ge(shift_loaded[s % 2], 16 * (STEPS // 2 * i + (s // 2 + 1)))
                    need = 4 * (PER * i + t) + (q - 1)
                    if positive(need):
                        pe.wait_ge(exp_done, need)
                    for e in range(2):
                        h = 2 * (q % 2) + e
                        last = pe.matmul(banks[:, 2 * (q % 2) + e, :], K[0:ROWS, buf, h, j * P:(j + 1) * P],
                                         Q[0:ROWS, buf, c, h * N:(h + 1) * N], start=True, stop=True)
                    last.then_inc(scores_ready, 1)

                def values(i, t, jj):
                    if t < 0 and first(i):
                        return
                    s, p = t // PAIRS, t % PAIRS
                    if jj == 0:
                        pe.wait_ge(exp_done, 4 * (PER * i + t) + 4)
                        if p == 0:
                            need = STEPS * i + s
                            if positive(need):
                                pe.wait_ge(o_copied, need)
                    for h in range(HG):
                        last = pe.matmul(banks[h * W:(h + 1) * W, 6, :], V[:, s // QC % 2, 2 * p + jj, h * W:(h + 1) * W],
                                         probs[:, t % 2, jj, h, :], start=(p == 0 and jj == 0),
                                         stop=(p == PAIRS - 1 and jj == 1))
                    if jj == 1:
                        last.then_inc(pv_done, 1)

                def denominators(i, t):
                    if t < 0 and first(i):
                        return
                    s, p = t // PAIRS, t % PAIRS
                    pe.wait_ge(pair_sum_done, PER * i + (t + 1))
                    if p == 0:
                        need = STEPS * i + s
                        if positive(need):
                            pe.wait_ge(den_copied, need)
                    for h in range(HG):
                        last = pe.matmul(banks[h * W:(h + 1) * W, 7, :], ones[:], pair_sum[:, t % 2, h, :],
                                         start=(p == 0), stop=(p == PAIRS - 1))
                    last.then_inc(den_done, 1)

                def turn(i, last):
                    for t in range(PER):
                        todo = slots_of(t // PAIRS, t % PAIRS, last)
                        for step, slots in ((lambda: scores(i, t, 0), todo[0:1]),
                                            (lambda: scores(i, t, 1), todo[1:2]),
                                            (lambda: values(i, t - 1, 0), todo[2:4]),
                                            (lambda: scores(i, t, 2), todo[4:5]),
                                            (lambda: scores(i, t, 3), todo[5:6]),
                                            (lambda: values(i, t - 1, 1), todo[6:7]),
                                            (lambda: denominators(i, t - 2), todo[7:])):
                            step()
                            for when in slots:
                                slot(i, *when)

                pe.wait_ge(consts_ready, 4)
                for when in OPENING:
                    slot(0, *when)
                turns(pe, turn)
                values(TURNS - 1, PER - 1, 0)
                values(TURNS - 1, PER - 1, 1)
                denominators(TURNS - 1, PER - 2)
                denominators(TURNS - 1, PER - 1)


def ffn(nc, ident, banks, x, s_heads, s_den, g_attn, g_ffn, m1, m2, mb, b2, w1_h, w1_l, w2_h, w2_l, out):
    ITEMS = ST * (DFF // N)
    QT = DFF // N
    CHUNKS = 2
    PER = CHUNKS * ITEMS
    AT_X1 = 1
    AT_NT = AT_X1 + ST
    AT_LR = AT_NT + KT
    PREPS = AT_LR + 1
    GB = N // D2
    RT = N // P
    BIAS_HI, BIAS_LO = 0, W
    with ExitStack() as ctx:
        def sb(name, shape, dt):
            return ctx.enter_context(nc.sbuf_tensor(name, shape, dt))

        def sem(name):
            return ctx.enter_context(nc.semaphore(name))

        x_f = sb("c_x", [P, 2, ST, D], F32)
        heads = sb("c_heads", [P, 2, GROUPS, N], F32)
        den = sb("c_den", [P, 2, N], F32)
        scale = sb("scale", [P, 2, ST, H], F32)
        x1 = sb("x1", [P, 2, ST, D], F32)
        xn = sb("c_xn", [P, ST, D], F32)
        xT_h = sb("c_xT_h", [P, 2, KT, N], F16)
        xT_l = sb("c_xT_l", [P, 2, KT, N], F16)
        lr_h = sb("lr_h", [P, 2, N], F16)
        lr_l = sb("lr_l", [P, 2, N], F16)
        peak = sb("peak", [P, 2, GB], F32)
        is_peak = sb("is_peak", [P, 2, N], F32)
        goes_on = sb("goes_on", [P, N], F32)
        count = sb("count", [P, 2, N], F32)
        relu = sb("relu", [P, 2, N], F32)
        act_f = sb("act_f", [P, 2, N], F32)
        aT_h = sb("aT_h", [P, 2, RT, P], F16)
        aT_l = sb("aT_l", [P, 2, RT, P], F16)
        result = sb("result", [P, 2, D], F32)
        gate = sb("gate", [P, 2, 2], F32)
        b2_f = sb("b2_f", [P, D], F32)
        b2_g = sb("b2_g", [P, D], F32)
        m1_f = sb("m1_f", [P, KT, 2 * DL], F32)
        m1_h = sb("m1_h", [P, KT, 2 * DL], F16)
        m1_l = sb("m1_l", [P, KT, 2 * DL], F16)
        m2_f = sb("m2_f", [P, DFF], F32)
        mb_f = sb("mb_f", [2 * W, DFF], F32)
        mb_h = sb("mb_h", [2 * W, DFF], F16)
        m2_1 = sb("m2_1", [P, DFF], F16)
        m2_2 = sb("m2_2", [P, DFF], F16)
        stats = sb("c_stats", [P, ST, 6], F32)
        moments = sb("c_moments", [P, 3, ST], F32)
        small = sb("c_small", [P, 5, ST], F32)

        consts_loaded = sem("c_consts_loaded")
        den_cleared = sem("den_cleared")
        zeros_ready = sem("zeros_ready")
        consts_hi = sem("c_consts_hi")
        consts_ready = sem("c_consts_ready")
        rows_loaded = [sem(f"rows_loaded{i}") for i in range(2)]
        prep_filled = sem("prep_filled")
        prep_hi = sem("prep_hi")
        prep_free = sem("prep_free")
        ln_step = sem("c_ln_step")
        sqrt_done = sem("c_sqrt_done")
        logits_filled = sem("logits_filled")
        mid_filled = sem("mid_filled")
        aT_filled = sem("aT_filled")
        w2_done = sem("w2_done")
        peak_done = sem("peak_done")
        is_peak_done = sem("is_peak_done")
        count_done = sem("count_done")
        relu_done = sem("relu_done")
        act_done = sem("act_done")
        aT_hi_done = sem("aT_hi_done")
        aT_lo_done = sem("aT_lo_done")
        inverted = sem("inverted")
        x1_done = sem("x1_done")
        biased = sem("biased")
        result_ready = sem("result_ready")
        result_stored = [sem(f"result_stored{i}") for i in range(2)]

        LOADS = 1 + 2 * GROUPS
        PREP_BANK, Y_BANK = 7, 6

        def prep_at(t):
            return {0: [0, 1], 1: [2], 2: [3], 3: [4], 7: [5], 8: [6], 9: [7], 10: [8], 12: [9]}.get(t, [])

        NORM_AT = 4

        def turns(eng, body):
            body(0, False)
            with eng.Fori(1, B - 1) as i:
                body(i, False)
            body(B - 1, True)

        with nc.Block() as block:
            @block.sync
            def _(sp):
                def load_rows(i, c):
                    need = ST * (2 * i + (c - 1))
                    if positive(need):
                        sp.wait_ge(x1_done, need)
                    sp.dma_start(x_f[:, c % 2], x[bass.ds(i * SQ + c * N, N), :].rearrange("(s p) d -> p s d", p=P)
                                 ).then_inc(rows_loaded[c % 2], 16)
                    for g in range(GROUPS):
                        start = (c // 2 * GROUPS + g) * QC + c % 2
                        sp.dma_start(heads[:, c % 2, g, :], s_heads[bass.ds(i * (GROUPS * QC * P) + start * P, P), :]
                                     ).then_inc(rows_loaded[c % 2], 16)
                        sp.dma_start(den[g * HG:(g + 1) * HG, c % 2, :],
                                     s_den[bass.ds(i * (GROUPS * QC * HG) + start * HG, HG), :]
                                     ).then_inc(rows_loaded[c % 2], 16)

                def store(i, c, s):
                    n = ST * c + s
                    sp.wait_ge(result_ready, 2 * ST * i + (n + 1))
                    sp.dma_start(out[bass.ds(i * SQ + n * P, P), :], result[:, n % 2, :]
                                 ).then_inc(result_stored[n % 2], 16)

                def turn(i, last):
                    for c in range(CHUNKS):
                        for s in range(ST):
                            store(i, c, s)
                            if s == 0 and not last:
                                load_rows(i, c + 2)

                sp.dma_start(m1_f[:, :, 0:DL], m1.rearrange("(k p) l -> p k l", p=P)).then_inc(consts_loaded, 16)
                sp.dma_start(m1_f[:, :, DL:2 * DL], m1.rearrange("(k p) l -> p k l", p=P)).then_inc(consts_loaded, 16)
                for at in (0, DL):
                    sp.dma_start(m2_f[at:at + DL, :], m2).then_inc(consts_loaded, 16)
                for at in (BIAS_HI, BIAS_LO):
                    sp.dma_start(mb_f[at:at + 1, :], mb).then_inc(consts_loaded, 16)
                sp.dma_start(b2_f[:], b2.partition_broadcast(P)).then_inc(consts_loaded, 16)
                for n, g in enumerate((g_attn, g_ffn)):
                    sp.dma_start(gate[:, 0, n:n + 1], g.partition_broadcast(P)).then_inc(consts_loaded, 16)
                sp.wait_ge(den_cleared, 1)
                load_rows(0, 0)
                load_rows(0, 1)
                turns(sp, turn)
                for k in range(2):
                    sp.wait_ge(result_stored[k], 16 * (SQ // P * B // 2))

            @block.gpsimd
            def _(pool):
                pool.memset(den[:], 0.0).then_inc(den_cleared, 1)
                pool.memset(m2_2[0:DL, :], 0.0).then_inc(zeros_ready, 1)
                pool.memset(lr_l[:], 1.0).then_inc(zeros_ready, 1)
                pool.memset(goes_on[:], 1.0).then_inc(zeros_ready, 1)
                pool.wait_ge(zeros_ready, 3)
                pool.memset(goes_on[:].rearrange("p (g d) -> p g d", d=D2)[:, :, 0:1], 0.0).then_inc(zeros_ready, 1)

                def add(i, c, s):
                    need = ST * (2 * i + (c - 1))
                    if positive(need):
                        pool.wait_ge(result_ready, need)
                    pool.wait_ge(rows_loaded[c % 2], 16 * LOADS * (i + (c // 2 + 1)))
                    pool.wait_ge(prep_free, PREPS * (2 * i + c) + (AT_X1 + s + 1))
                    pool.tensor_tensor(x1[:, c % 2, s, :], xn[:, s, :], x_f[:, c % 2, s, :], ALU.add
                                       ).then_inc(x1_done, 1)

                def bias(i, c):
                    pool.wait_ge(ln_step, LN_STEPS * (2 * i + (c + 1)))
                    pool.wait_ge(x1_done, ST * (2 * i + (c + 1)))
                    pool.tensor_tensor(x1[:, c % 2], x1[:, c % 2], b2_g[:].unsqueeze(1).to_broadcast([P, ST, D]), ALU.add
                                       ).then_inc(biased, 1)

                def turn(i, last):
                    for c in range(CHUNKS):
                        if last and c == 1:
                            continue
                        for s in range(ST):
                            add(i, c + 1, s)
                        bias(i, c + 1)

                for s in range(ST):
                    add(0, 0, s)
                pool.wait_ge(consts_ready, 4)
                bias(0, 0)
                turns(pool, turn)

            @block.scalar
            def _(act):
                def prep(i, c, n):
                    C = 2 * i + c
                    bank = banks[:, PREP_BANK, :]
                    if n < AT_NT:
                        return
                    act.wait_ge(prep_filled, PREPS * C + (n + 1))
                    to = xT_h[:, c % 2, n - AT_NT, :] if n < AT_LR else lr_h[:, c % 2, :]
                    act.activation(to, bank, ACT.Copy).then_inc(prep_hi, 1)

                def item(i, u):
                    U = PER * i + u
                    if isinstance(U, int) and U < 0:
                        return
                    act.wait_ge(aT_filled, U + 1)
                    need = U - 1
                    if positive(need):
                        act.wait_ge(w2_done, need)
                    act.activation(aT_h[:, u % 2].rearrange("p f t -> p (f t)"), banks[:, 4 + u % 2, :], ACT.Copy
                                   ).then_inc(aT_hi_done, 1)

                def turn(i, last):
                    for u in range(PER):
                        item(i, u - 1)
                        c, t = divmod(u, ITEMS)
                        if last and c == 1:
                            continue
                        for n in prep_at(t):
                            prep(i, c + 1, n)
                        if t == NORM_AT:
                            scalar_layer_norm(act, 2 * i + (c + 1), small, sqrt_done, ln_step)

                act.wait_ge(consts_loaded, 16 * 9)
                act.activation(gate[:, 1, :], gate[:, 0, :], ACT.Tanh).then_inc(consts_hi, 1)
                act.activation(m1_h[:], m1_f[:], ACT.Copy).then_inc(consts_hi, 1)
                act.activation(m2_1[0:DL, :], m2_f[0:DL, :], ACT.Copy).then_inc(consts_hi, 1)
                act.activation(m2_2[DL:2 * DL, :], m2_f[DL:2 * DL, :], ACT.Copy).then_inc(consts_hi, 1)
                act.activation(mb_h[BIAS_LO:BIAS_LO + 1, :], mb_f[BIAS_LO:BIAS_LO + 1, :], ACT.Copy).then_inc(consts_hi, 1)
                act.wait_ge(zeros_ready, 4)
                act.activation(m2_2[BIAS_HI:BIAS_HI + 1, :], mb_f[BIAS_HI:BIAS_HI + 1, :], ACT.Copy).then_inc(consts_hi, 1)
                scalar_layer_norm(act, 0, small, sqrt_done, ln_step)
                for n in range(PREPS):
                    prep(0, 0, n)
                turns(act, turn)
                item(0, PER * B - 1)

            @block.vector
            def _(dve):
                def prep(i, c, n):
                    C = 2 * i + c
                    bank = banks[:, PREP_BANK, :]
                    if n < AT_NT:
                        dve.wait_ge(prep_filled, PREPS * C + (n + 1))
                    if n == 0:
                        dve.reciprocal(scale[:, 0], bank.rearrange("p (s c) -> p s c", c=P)[:, :, 0:H]).then_inc(inverted, 1)
                        dve.wait_ge(inverted, C + 1)
                        ins = dve.tensor_scalar(scale[:, 1].rearrange("p s h -> p (s h)"),
                                                scale[:, 0].rearrange("p s h -> p (s h)"), gate[:, 1, 0:1], None,
                                                ALU.mult)
                    elif n < AT_NT:
                        if n == AT_X1:
                            dve.wait_ge(prep_free, PREPS * C + AT_X1)
                        s = n - AT_X1
                        dve.tensor_tensor(xn[:, s, :].rearrange("p (h w) -> p h w", w=W),
                                          bank.rearrange("p (h w) -> p h w", w=W),
                                          scale[:, 1, s, :].unsqueeze(2).to_broadcast([P, H, W]), ALU.mult
                                          ).then_inc(prep_free, 1)
                        return
                    else:
                        dve.wait_ge(prep_hi, (KT + 1) * C + (n - AT_NT + 1))
                        if n < AT_LR:
                            ins = dve.tensor_tensor(xT_l[:, c % 2, n - AT_NT, :], bank, xT_h[:, c % 2, n - AT_NT, :],
                                                    ALU.subtract)
                        else:
                            ins = dve.tensor_tensor(lr_l[DL:2 * DL, c % 2, :], bank[DL:2 * DL, :],
                                                    lr_h[DL:2 * DL, c % 2, :], ALU.subtract)
                    ins.then_inc(prep_free, 1)

                def norm(i, c):
                    dve.wait_ge(x1_done, ST * (2 * i + (c + 1)))
                    vector_layer_norm(dve, 2 * i + c, x1[:, c % 2], xn, stats, moments, small, sqrt_done, ln_step)

                def lo_part(i, u):
                    U = PER * i + u
                    if isinstance(U, int) and U < 0:
                        return
                    dve.wait_ge(aT_hi_done, U + 1)
                    dve.tensor_tensor(aT_l[:, u % 2].rearrange("p f t -> p (f t)"), banks[:, 4 + u % 2, :],
                                      aT_h[:, u % 2].rearrange("p f t -> p (f t)"), ALU.subtract
                                      ).then_inc(aT_lo_done, 1)

                def finish(i, u):
                    U = PER * i + u
                    if (isinstance(U, int) and U < 0) or u % QT != QT - 1:
                        return
                    r = u // QT % (2 * ST)
                    dve.wait_ge(w2_done, U + 1)
                    dve.wait_ge(biased, 2 * i + (u // (QT * ST) + 1))
                    need = 16 * (ST * i + u // QT // 2)
                    if positive(need):
                        dve.wait_ge(result_stored[r % 2], need)
                    dve.scalar_tensor_tensor(result[:, r % 2, :], banks[:, Y_BANK, :], gate[:, 1, 1:2],
                                             x1[:, r // ST, r % ST, :], ALU.mult, ALU.add).then_inc(result_ready, 1)

                def item(i, u):
                    U = PER * i + u
                    par = u % 2
                    logits = banks[:, par, :].rearrange("p (g d) -> p g d", d=D2)
                    dve.wait_ge(logits_filled, U + 1)
                    dve.tensor_reduce(peak[:, par, :], logits, AX_X, ALU.max).then_inc(peak_done, 1)
                    dve.wait_ge(peak_done, U + 1)
                    dve.tensor_tensor(is_peak[:, par, :].rearrange("p (g d) -> p g d", d=D2), logits,
                                      peak[:, par, :].unsqueeze(2).to_broadcast([P, GB, D2]), ALU.is_equal
                                      ).then_inc(is_peak_done, 1)
                    dve.wait_ge(is_peak_done, U + 1)
                    dve.tensor_tensor_scan(count[:, par, :], goes_on[:], is_peak[:, par, :], 0.0, ALU.mult, ALU.add
                                           ).then_inc(count_done, 1)
                    dve.wait_ge(mid_filled, U + 1)
                    dve.scalar_tensor_tensor(relu[:, par, :], banks[:, 2 + par, :], 0.0, is_peak[:, par, :],
                                             ALU.max, ALU.mult).then_inc(relu_done, 1)
                    lo_part(i, u - 1)
                    dve.wait_ge(count_done, U + 1)
                    dve.wait_ge(relu_done, U + 1)
                    need = U - 1
                    if positive(need):
                        dve.wait_ge(aT_filled, need)
                    dve.scalar_tensor_tensor(act_f[:, par, :], count[:, par, :], 1.0, relu[:, par, :],
                                             ALU.is_equal, ALU.mult).then_inc(act_done, 1)

                def turn(i, last):
                    for u in range(PER):
                        item(i, u)
                        finish(i, u - 3)
                        c, t = divmod(u, ITEMS)
                        if last and c == 1:
                            continue
                        for n in prep_at(t):
                            prep(i, c + 1, n)
                        if t == NORM_AT:
                            norm(i, c + 1)

                dve.wait_ge(consts_hi, 6)
                dve.tensor_tensor(m1_l[:], m1_f[:], m1_h[:], ALU.subtract).then_inc(consts_ready, 1)
                dve.tensor_tensor(m2_1[DL:2 * DL, :], m2_f[DL:2 * DL, :], m2_2[DL:2 * DL, :], ALU.subtract
                                  ).then_inc(consts_ready, 1)
                dve.tensor_tensor(m2_2[BIAS_LO:BIAS_LO + 1, :], mb_f[BIAS_LO:BIAS_LO + 1, :],
                                  mb_h[BIAS_LO:BIAS_LO + 1, :], ALU.subtract).then_inc(consts_ready, 1)
                dve.tensor_scalar(b2_g[:], b2_f[:], gate[:, 1, 1:2], None, ALU.mult).then_inc(consts_ready, 1)
                dve.wait_ge(zeros_ready, 4)
                for n in range(AT_NT):
                    prep(0, 0, n)
                norm(0, 0)
                for n in range(AT_NT, PREPS):
                    prep(0, 0, n)
                turns(dve, turn)
                lo_part(0, PER * B - 1)
                for u in range(PER * B - 3, PER * B):
                    finish(0, u)

            @block.tensor
            def _(pe):
                def prep(i, c, n):
                    C = 2 * i + c
                    bank = banks[:, PREP_BANK, :]
                    need = PREPS * C + n
                    if positive(need):
                        pe.wait_ge(prep_free, need)
                    if n == 0:
                        pe.wait_ge(rows_loaded[c % 2], 16 * LOADS * (i + (c // 2 + 1)))
                        for s in range(ST):
                            last = pe.transpose(bank[:, s * P:(s + 1) * P], den[:, c % 2, s * P:(s + 1) * P], ident[:])
                    elif n < AT_NT:
                        for g in range(GROUPS):
                            last = pe.transpose(bank[:, g * P:(g + 1) * P], heads[:, c % 2, g, (n - AT_X1) * P:(n - AT_X1 + 1) * P],
                                                ident[:])
                    elif n < AT_LR:
                        k = n - AT_NT
                        if k == 0:
                            pe.wait_ge(ln_step, LN_STEPS * (C + 1))
                        for s in range(ST):
                            last = pe.transpose(bank[:, s * P:(s + 1) * P], xn[:, s, k * P:(k + 1) * P], ident[:])
                    else:
                        last = pair_product(pe, bank, lambda k: (m1_h[:, k, :], m1_l[:, k, :]),
                                            lambda k: (xT_h[:, c % 2, k, :], xT_l[:, c % 2, k, :]))
                    last.then_inc(prep_filled, 1)

                def item(i, u):
                    U = PER * i + u
                    c, t = divmod(u, ITEMS)
                    s, q = divmod(t, QT)
                    rows, cols = slice(s * P, (s + 1) * P), slice(q * N, (q + 1) * N)
                    if t == 0:
                        pe.wait_ge(prep_free, PREPS * (2 * i + (c + 1)))
                    need = U - 1
                    if positive(need):
                        pe.wait_ge(is_peak_done, need)
                    logits = banks[:, u % 2, :]
                    pe.matmul(logits, lr_h[:, c, rows], m2_1[:, cols], start=True, stop=False)
                    pe.matmul(logits, lr_l[:, c, rows], m2_2[:, cols], start=False, stop=True
                              ).then_inc(logits_filled, 1)
                    need = U - 1
                    if positive(need):
                        pe.wait_ge(relu_done, need)
                    pair_product(pe, banks[:, 2 + u % 2, :], lambda k: (xT_h[:, c, k, rows], xT_l[:, c, k, rows]),
                                 lambda k: (w1_h[:, k, cols], w1_l[:, k, cols])).then_inc(mid_filled, 1)

                def turn_back(i, u):
                    U = PER * i + u
                    if isinstance(U, int) and U < 0:
                        return
                    pe.wait_ge(act_done, U + 1)
                    need = U - 1
                    if positive(need):
                        pe.wait_ge(aT_lo_done, need)
                    for a in range(RT):
                        last = pe.transpose(banks[:, 4 + u % 2, a * P:(a + 1) * P],
                                            act_f[:, u % 2, a * P:(a + 1) * P], ident[:])
                    last.then_inc(aT_filled, 1)

                def second(i, u):
                    U = PER * i + u
                    if isinstance(U, int) and U < 0:
                        return
                    q = u % QT
                    pe.wait_ge(aT_lo_done, U + 1)
                    if q == 0:
                        need = 2 * ST * i + u // QT
                        if positive(need):
                            pe.wait_ge(result_ready, need)
                    pair_product(pe, banks[:, Y_BANK, :], lambda a: (aT_h[:, u % 2, a, :], aT_l[:, u % 2, a, :]),
                                 lambda a: (w2_h[:, q * RT + a, :], w2_l[:, q * RT + a, :]), range(RT),
                                 start=(q == 0), stop=(q == QT - 1)).then_inc(w2_done, 1)

                def turn(i, last):
                    for u in range(PER):
                        item(i, u)
                        turn_back(i, u - 1)
                        second(i, u - 2)
                        c, t = divmod(u, ITEMS)
                        if last and c == 1:
                            continue
                        for n in prep_at(t):
                            prep(i, c + 1, n)

                pe.wait_ge(consts_ready, 4)
                for n in range(PREPS):
                    prep(0, 0, n)
                turns(pe, turn)
                turn_back(0, PER * B - 1)
                second(0, PER * B - 2)
                second(0, PER * B - 1)


def build(nc, x, ctxT, mask, g_attn, g_ffn, WqT, bq, WkT, bk, WvT, bv, m1, m2, mb, w1, w2, b2, out):
    s_K = [nc.dram_tensor(f"s_K{n}", (B * D, SKV), F16).ap() for n in "hl"]
    s_Q = [nc.dram_tensor(f"s_Q{n}", (B * D, SQ), F16).ap() for n in "hl"]
    s_V = nc.dram_tensor("s_V", (UNITS * SKV, P), F32).ap()
    s_mask = nc.dram_tensor("s_mask", (UNITS, SKV), F16).ap()
    s_heads = nc.dram_tensor("s_heads", (UNITS * QC * P, N), F32).ap()
    s_den = nc.dram_tensor("s_den", (UNITS * QC * HG, N), F32).ap()
    with ExitStack() as ctx:
        ident = ctx.enter_context(nc.sbuf_tensor("ident", [P, P], F32))
        banks = ctx.enter_context(nc.psum_tensor("banks", [P, BANKS, N], F32))
        project(nc, ident, banks, x, ctxT, mask, WqT, WkT, WvT, bq, bk, bv, s_K, s_Q, s_V, s_mask)
        w1_h, w1_l = (ctx.enter_context(nc.sbuf_tensor(f"w1_{n}", [P, KT, DFF], F16)) for n in "hl")
        w2_h, w2_l = (ctx.enter_context(nc.sbuf_tensor(f"w2_{n}", [P, FT, D], F16)) for n in "hl")
        attend(nc, ident, banks, s_K, s_Q, s_V, s_mask, s_heads, s_den, w1, w2, w1_h, w1_l, w2_h, w2_l)
        ffn(nc, ident, banks, x, s_heads, s_den, g_attn, g_ffn, m1, m2, mb, b2, w1_h, w1_l, w2_h, w2_l, out)


def kernel(x, ctx_1024, mask_BxS2_ik0, g_xattn, g_ffn, L0_xattn_Wq, L0_xattn_bq, L0_xattn_Wk, L0_xattn_bk,
           L0_xattn_Wv, L0_xattn_bv, L0_ffn_m1, L0_ffn_m2, L0_ffn_mb, L0_ffn_w1, L0_ffn_w2, L0_ffn_b2):
    import numpy as _np
    import concourse.bacc as _bacc
    from concourse import mybir as _mybir
    from concourse.bass_utils import run_bass_kernel_spmd as _run

    a = _np.asarray
    laid_out = {
        "x": a(x).reshape(B * SQ, D),
        "ctxT": a(ctx_1024).transpose(0, 2, 1).reshape(B * D, SKV),
        "mask": a(mask_BxS2_ik0).repeat(GROUPS, axis=0),
        "g_attn": a(g_xattn),
        "g_ffn": a(g_ffn),
        "WqT": a(L0_xattn_Wq).T,
        "bq": a(L0_xattn_bq).reshape(KT, P).T,
        "WkT": a(L0_xattn_Wk).T,
        "bk": a(L0_xattn_bk).reshape(KT, P).T,
        "WvT": a(L0_xattn_Wv).T,
        "bv": a(L0_xattn_bv),
        "m1": a(L0_ffn_m1),
        "m2": a(L0_ffn_m2).reshape(DL, DFF),
        "mb": a(L0_ffn_mb).reshape(1, DFF),
        "w1": a(L0_ffn_w1).reshape(D, DFF),
        "w2": a(L0_ffn_w2).transpose(1, 0, 2).reshape(DFF, D),
        "b2": a(L0_ffn_b2),
    }
    nc = _bacc.Bacc("TRN2", target_bir_lowering=False, num_devices=1)
    arrays, args = {}, []
    for name, value in laid_out.items():
        value = _np.ascontiguousarray(value)
        arrays[f"in_{name}"] = value
        args.append(nc.dram_tensor(f"in_{name}", value.shape, _mybir.dt.from_np(value.dtype), kind="ExternalInput").ap())
    out = nc.dram_tensor("out_x", (B * SQ, D), _mybir.dt.float32, kind="ExternalOutput").ap()
    build(nc, *args, out)
    r = _run(nc, [arrays], core_ids=[0])
    return r.results[0]["out_x"].reshape(B, SQ, D)
```

```python
from contextlib import ExitStack

import concourse.bass as bass
from concourse import mybir

F32 = mybir.dt.float32
F16 = mybir.dt.float16
I32 = mybir.dt.int32
ACT = mybir.ActivationFunctionType
ALU = mybir.AluOpType
AX_X = mybir.AxisListType.X

P = 128
B, SQ, SKV, D, H = 4, 1024, 2048, 512, 16
W = D // H
SCALE = float(W) ** -0.5
MASKED = 10000.0
EPS = 1e-5
D1, D2 = 32, 64
DFF = D1 * D2
DL = 64
KT = D // P
FT = DFF // P
N = 512
BANKS = 8
HG = P // W
GROUPS = H // HG
UNITS = B * GROUPS
QC = SQ // N
CC = SKV // N
JT = SKV // P
ST = N // P
LN_STEPS = 10


def positive(value):
    return not isinstance(value, int) or value > 0


def norm_statistics(dve, n, moments, stats, small, step):
    base = LN_STEPS * n
    var_eps, root, inv, tmp, rstd = (small[:, k, :] for k in range(5))
    total, gap, mean = (moments[:, k, :] for k in range(3))
    dve.wait_ge(step, base + 1)
    dve.tensor_tensor(total, stats[:, :, 1], stats[:, :, 4], ALU.add)
    dve.tensor_tensor(gap, stats[:, :, 1], stats[:, :, 4], ALU.subtract)
    dve.tensor_tensor(tmp, stats[:, :, 2], stats[:, :, 5], ALU.add).then_inc(step, 1)
    dve.wait_ge(step, base + 2)
    dve.tensor_scalar(mean, total, 0.5, None, ALU.mult)
    dve.tensor_tensor(inv, gap, gap, ALU.mult)
    dve.tensor_scalar(rstd, tmp, 1.0 / D, EPS, ALU.mult, ALU.add).then_inc(step, 1)
    dve.wait_ge(step, base + 3)
    dve.scalar_tensor_tensor(var_eps, inv, 0.25, rstd, ALU.mult, ALU.add).then_inc(step, 1)


def norm_scale(dve, n, small, sqrt_done, step):
    base = LN_STEPS * n
    var_eps, root, inv, tmp, rstd = (small[:, k, :] for k in range(5))
    dve.wait_ge(sqrt_done, n + 1)
    dve.reciprocal(inv, root).then_inc(step, 1)
    dve.wait_ge(step, base + 5)
    dve.tensor_tensor(tmp, inv, inv, ALU.mult).then_inc(step, 1)
    dve.wait_ge(step, base + 6)
    dve.tensor_tensor(rstd, tmp, var_eps, ALU.mult).then_inc(step, 1)
    dve.wait_ge(step, base + 7)
    dve.tensor_scalar(tmp, rstd, -0.5, 1.5, ALU.mult, ALU.add).then_inc(step, 1)
    dve.wait_ge(step, base + 8)
    dve.tensor_tensor(rstd, inv, tmp, ALU.mult).then_inc(step, 1)


def norm_apply(dve, n, rows, out, moments, small, step, tiles):
    mean, rstd = moments[:, 2, :], small[:, 4, :]
    dve.wait_ge(step, LN_STEPS * n + 9)
    for s in tiles:
        last = dve.tensor_scalar(out[:, s, :], rows[:, s, :], mean[:, s:s + 1], rstd[:, s:s + 1],
                                 ALU.subtract, ALU.mult)
    if tiles[-1] == ST - 1:
        last.then_inc(step, 1)


def vector_layer_norm(dve, n, rows, out, stats, moments, small, sqrt_done, step):
    for s in range(ST):
        last = dve.bn_stats(stats[:, s, :], rows[:, s, :])
    last.then_inc(step, 1)
    norm_statistics(dve, n, moments, stats, small, step)
    norm_scale(dve, n, small, sqrt_done, step)
    norm_apply(dve, n, rows, out, moments, small, step, range(ST))


def scalar_layer_norm(act, n, small, sqrt_done, step):
    act.wait_ge(step, LN_STEPS * n + 4)
    act.activation(small[:, 1, :], small[:, 0, :], ACT.Sqrt).then_inc(sqrt_done, 1)


def pair_product(pe, out, left, right, tiles=range(KT), start=True, stop=True):
    for k in tiles:
        (lh, ll), (rh, rl) = left(k), right(k)
        pe.matmul(out, lh, rh, start=start and k == tiles[0], stop=False)
        pe.matmul(out, lh, rl, start=False, stop=False)
        last = pe.matmul(out, ll, rh, start=False, stop=stop and k == tiles[-1])
    return last


def project(nc, ident, banks, x, ctxT, mask, WqT, WkT, WvT, bq, bk, bv, s_K, s_Q, s_V, s_mask, s_ones):
    with ExitStack() as ctx:
        def sb(name, shape, dt):
            return ctx.enter_context(nc.sbuf_tensor(name, shape, dt))

        def sem(name):
            return ctx.enter_context(nc.semaphore(name))

        w_f = [sb(f"w{n}_f", [P, KT, D], F32) for n in "qkv"]
        w_h = [sb(f"w{n}_h", [P, KT, D], F16) for n in "qkv"]
        w_l = [sb(f"w{n}_l", [P, KT, D], F16) for n in "qkv"]
        bq_f = sb("bq_f", [P, KT], F32)
        bq_s = sb("bq_s", [P, KT], F32)
        bk_f = sb("bk_f", [P, KT], F32)
        bv_f = sb("bv_f", [P, D], F32)
        mask_i = sb("mask_i", [UNITS, SKV], I32)
        mask_h = sb("mask_h", [UNITS, SKV], F16)
        ones_h = sb("ones_h", [UNITS, N], F16)
        ctx_f = sb("ctx_f", [P, 2, KT, N], F32)
        ctx_h = sb("ctx_h", [P, 2, KT, N], F16)
        ctx_l = sb("ctx_l", [P, 2, KT, N], F16)
        k_h = sb("k_h", [P, 2, KT, N], F16)
        k_l = sb("k_l", [P, 2, KT, N], F16)
        v_f = sb("v_f", [P, 2, ST, D], F32)
        x_f = sb("x_f", [P, QC, ST, D], F32)
        xn = sb("xn", [P, ST, D], F32)
        xT_h = sb("xT_h", [P, KT, N], F16)
        xT_l = sb("xT_l", [P, KT, N], F16)
        q_h = sb("q_h", [P, QC, KT, N], F16)
        q_l = sb("q_l", [P, QC, KT, N], F16)
        stats = sb("stats", [P, ST, 6], F32)
        moments = sb("moments", [P, 3, ST], F32)
        small = sb("small", [P, 5, ST], F32)

        weights_loaded = [sem(f"w{n}_loaded") for n in "qkv"]
        consts_loaded = sem("consts_loaded")
        wq_scaled = sem("wq_scaled")
        weights_hi = sem("weights_hi")
        weights_ready = sem("weights_ready")
        ones_ready = sem("ones_ready")
        ones_stored = sem("ones_stored")
        mask_ready = sem("mask_ready")
        mask_stored = sem("mask_stored")
        ctx_loaded = [sem(f"ctx_loaded{i}") for i in range(2)]
        ctx_hi_done = sem("ctx_hi_done")
        ctx_lo_done = sem("ctx_lo_done")
        x_loaded = [sem(f"x_loaded{i}") for i in range(QC)]
        ln_step = sem("ln_step")
        sqrt_done = sem("sqrt_done")
        bank_filled = sem("bank_filled")
        hi_done = sem("hi_done")
        bank_free = sem("bank_free")
        kv_stored = [sem(f"kv_stored{i}") for i in range(2)]
        q_stored = [sem(f"q_stored{i}") for i in range(QC)]
        ident_zero = sem("ident_zero")
        ident_ready = sem("ident_ready")

        JOBS = [("KV", 0), ("T", 0), ("KV", 1), ("Q", 0), ("T", 1), ("KV", 2), ("Q", 1), ("KV", 3)]
        SIZE = {"KV": KT + ST, "T": KT, "Q": KT}
        HIS = KT
        first, at = {}, 0
        for job in JOBS:
            first[job] = at
            at += SIZE[job[0]]
        PER = at
        assert PER % BANKS == 0
        KV_DMAS = 2 + GROUPS

        def through(b, job):
            return PER * b + (first[job] + SIZE[job[0]])

        def before_T(b, c):
            return through(b, ("Q", 0)) if c else through(b - 1, ("Q", 1))

        with nc.Block() as block:
            @block.sync
            def _(sp):
                for n, w in ((1, WkT), (2, WvT)):
                    sp.dma_start(w_f[n][:], w.rearrange("(k p) o -> p k o", p=P)).then_inc(weights_loaded[n], 16)
                sp.dma_start(bq_f[:], bq).then_inc(consts_loaded, 16)
                sp.dma_start(bk_f[:], bk).then_inc(consts_loaded, 16)
                sp.dma_start(bv_f[:], bv.partition_broadcast(P)).then_inc(consts_loaded, 16)
                sp.dma_start(mask_i[:], mask).then_inc(consts_loaded, 16)
                sp.dma_start(w_f[0][:], WqT.rearrange("(k p) o -> p k o", p=P)).then_inc(weights_loaded[0], 16)
                sp.wait_ge(ones_ready, 1)
                sp.dma_start(s_ones, ones_h[:]).then_inc(ones_stored, 16)
                sp.wait_ge(mask_ready, 1)
                sp.dma_start(s_mask, mask_h[:]).then_inc(mask_stored, 16)

                def batch(b):
                    for kind, c in JOBS:
                        if kind == "KV":
                            sp.wait_ge(bank_free, through(b, (kind, c)))
                            for s_k, k in zip(s_K, (k_h, k_l)):
                                sp.dma_start(
                                    s_k[bass.ds(b * D, D), c * N:(c + 1) * N].rearrange("(m p) t -> p m t", p=P),
                                    k[:, c % 2]).then_inc(kv_stored[c % 2], 16)
                            for g in range(GROUPS):
                                sp.dma_start(
                                    s_V[bass.ds(b * (GROUPS * SKV) + (g * SKV + c * N), N), :].rearrange(
                                        "(s p) e -> p s e", p=P),
                                    v_f[:, c % 2, :, g * P:(g + 1) * P]).then_inc(kv_stored[c % 2], 16)
                        if kind == "Q":
                            sp.wait_ge(bank_free, through(b, (kind, c)))
                            for s_q, q in zip(s_Q, (q_h, q_l)):
                                sp.dma_start(
                                    s_q[bass.ds(b * D, D), c * N:(c + 1) * N].rearrange("(m p) t -> p m t", p=P),
                                    q[:, c]).then_inc(q_stored[c], 16)

                batch(0)
                with sp.Fori(1, B) as b:
                    batch(b)
                sp.wait_ge(ones_stored, 16)
                sp.wait_ge(mask_stored, 16)
                for i in range(2):
                    sp.wait_ge(kv_stored[i], 16 * KV_DMAS * B * CC // 2)
                    sp.wait_ge(q_stored[i], 16 * 2 * B)

            @block.gpsimd
            def _(pool):
                def load_ctx(b, c):
                    need = CC * b + (c - 1)
                    if positive(need):
                        pool.wait_ge(ctx_lo_done, need)
                    pool.dma_start(ctx_f[:, c % 2],
                                   ctxT[bass.ds(b * D, D), c * N:(c + 1) * N].rearrange("(k p) t -> p k t", p=P)
                                   ).then_inc(ctx_loaded[c % 2], 16)

                def load_x(b, c):
                    need = LN_STEPS * (QC * b + (c - 1))
                    if positive(need):
                        pool.wait_ge(ln_step, need)
                    pool.dma_start(x_f[:, c], x[bass.ds(b * SQ + c * N, N), :].rearrange("(s p) d -> p s d", p=P)
                                   ).then_inc(x_loaded[c], 16)

                def batch(b):
                    load_ctx(b, 0)
                    load_x(b, 0)
                    load_ctx(b, 1)
                    load_x(b, 1)
                    for c in range(CC):
                        pool.wait_ge(ctx_hi_done, CC * b + (c + 1))
                        pool.tensor_tensor(ctx_l[:, c % 2], ctx_f[:, c % 2], ctx_h[:, c % 2], ALU.subtract
                                           ).then_inc(ctx_lo_done, 1)
                        if c + 2 < CC:
                            load_ctx(b, c + 2)

                pool.memset(ident[:], 0.0).then_inc(ident_zero, 1)
                pool.wait_ge(ident_zero, 1)
                pool.affine_select(out=ident[:], in_=ident[:], compare_op=ALU.not_equal, fill=1.0, base=0,
                                   pattern=[[-1, P]], channel_multiplier=1).then_inc(ident_ready, 1)
                batch(0)
                with pool.Fori(1, B) as b:
                    batch(b)

            @block.scalar
            def _(act):
                def ctx_hi(b, c):
                    act.wait_ge(ctx_loaded[c % 2], 32 * b + 16 * (c // 2 + 1))
                    need = through(b, ("KV", c - 2)) if c >= 2 else through(b - 1, ("KV", c + 2))
                    if positive(need):
                        act.wait_ge(bank_filled, need)
                    act.activation(ctx_h[:, c % 2], ctx_f[:, c % 2], ACT.Copy).then_inc(ctx_hi_done, 1)

                def weight_hi(n):
                    act.activation(w_h[n][:], w_f[n][:], ACT.Copy).then_inc(weights_hi, 1)

                def batch(b):
                    ctx_hi(b, 0)
                    if isinstance(b, int):
                        act.wait_ge(weights_loaded[1], 16)
                        weight_hi(1)
                        act.wait_ge(weights_loaded[2], 16)
                        weight_hi(2)
                        act.wait_ge(wq_scaled, 2)
                        weight_hi(0)
                        act.wait_ge(consts_loaded, 64)
                    scalar_layer_norm(act, QC * b, small, sqrt_done, ln_step)
                    ctx_hi(b, 1)
                    for kind, c in JOBS:
                        for g in range(HIS):
                            if g == 0 and kind == "KV":
                                need = 16 * KV_DMAS * (2 * b + c // 2)
                                if positive(need):
                                    act.wait_ge(kv_stored[c % 2], need)
                            if g == 0 and kind == "Q":
                                need = 32 * b
                                if positive(need):
                                    act.wait_ge(q_stored[c], need)
                            if g == 0 and kind == "T":
                                need = before_T(b, c)
                                if positive(need):
                                    act.wait_ge(bank_filled, need)
                            n = first[(kind, c)] + g
                            src = banks[:, n % BANKS, :]
                            act.wait_ge(bank_filled, PER * b + (n + 1))
                            if kind == "KV":
                                ins = act.activation(k_h[:, c % 2, g, :], src, ACT.Identity, bias=bk_f[:, g:g + 1])
                            elif kind == "Q":
                                ins = act.activation(q_h[:, c, g, :], src, ACT.Identity, bias=bq_s[:, g:g + 1])
                            else:
                                ins = act.activation(xT_h[:, g, :], src, ACT.Copy)
                            ins.then_inc(hi_done, 1)
                        if (kind, c) == ("T", 0):
                            scalar_layer_norm(act, QC * b + 1, small, sqrt_done, ln_step)
                        if kind == "KV" and c < 2:
                            ctx_hi(b, c + 2)

                batch(0)
                with act.Fori(1, B) as b:
                    batch(b)

            @block.vector
            def _(dve):
                def norm(b, c):
                    dve.wait_ge(x_loaded[c], 16 * b + 16)
                    need = through(b, ("T", 0)) if c else through(b - 1, ("T", 1))
                    if positive(need):
                        dve.wait_ge(bank_filled, need)
                    vector_layer_norm(dve, QC * b + c, x_f[:, c], xn, stats, moments, small, sqrt_done, ln_step)

                def batch(b):
                    norm(b, 0)
                    for j, (kind, c) in enumerate(JOBS):
                        for g in range(SIZE[kind]):
                            n = first[(kind, c)] + g
                            src = banks[:, n % BANKS, :]
                            if g < HIS:
                                dve.wait_ge(hi_done, HIS * len(JOBS) * b + (HIS * j + g + 1))
                            else:
                                if g == HIS:
                                    need = 16 * KV_DMAS * (2 * b + c // 2)
                                    if positive(need):
                                        dve.wait_ge(kv_stored[c % 2], need)
                                dve.wait_ge(bank_filled, PER * b + (n + 1))
                            if kind == "KV" and g < HIS:
                                ins = dve.scalar_tensor_tensor(k_l[:, c % 2, g, :], src, bk_f[:, g:g + 1],
                                                               k_h[:, c % 2, g, :], ALU.add, ALU.subtract)
                            elif kind == "KV":
                                ins = dve.tensor_tensor(v_f[:, c % 2, g - HIS, :], src, bv_f[:], ALU.add)
                            elif kind == "Q":
                                ins = dve.scalar_tensor_tensor(q_l[:, c, g, :], src, bq_s[:, g:g + 1],
                                                               q_h[:, c, g, :], ALU.add, ALU.subtract)
                            else:
                                ins = dve.tensor_tensor(xT_l[:, g, :], src, xT_h[:, g, :], ALU.subtract)
                            ins.then_inc(bank_free, 1)
                        if (kind, c) == ("T", 0):
                            norm(b, 1)

                def weight_lo(n, count):
                    dve.wait_ge(weights_hi, count)
                    dve.tensor_tensor(w_l[n][:], w_f[n][:], w_h[n][:], ALU.subtract).then_inc(weights_ready, 1)

                dve.memset(ones_h[:], 1.0).then_inc(ones_ready, 1)
                dve.wait_ge(weights_loaded[1], 16)
                weight_lo(1, 1)
                dve.wait_ge(weights_loaded[2], 16)
                weight_lo(2, 2)
                dve.wait_ge(weights_loaded[0], 16)
                dve.tensor_scalar(w_f[0][:], w_f[0][:], SCALE, None, ALU.mult).then_inc(wq_scaled, 1)
                dve.wait_ge(consts_loaded, 64)
                dve.tensor_scalar(bq_s[:], bq_f[:], SCALE, None, ALU.mult).then_inc(wq_scaled, 1)
                dve.tensor_scalar(mask_h[:], mask_i[:], MASKED, -MASKED, ALU.mult, ALU.add).then_inc(mask_ready, 1)
                dve.wait_ge(wq_scaled, 2)
                weight_lo(0, 3)
                batch(0)
                with dve.Fori(1, B) as b:
                    batch(b)

            @block.tensor
            def _(pe):
                def weight(n, cols):
                    return lambda k: (w_h[n][:, k, cols], w_l[n][:, k, cols])

                def batch(b):
                    for kind, c in JOBS:
                        if kind == "KV":
                            pe.wait_ge(ctx_lo_done, CC * b + (c + 1))
                        elif kind == "T":
                            pe.wait_ge(ln_step, LN_STEPS * (QC * b + (c + 1)))
                        else:
                            pe.wait_ge(bank_free, through(b, ("T", c)))
                        if isinstance(b, int) and kind == "Q" and c == 0:
                            pe.wait_ge(weights_ready, 3)
                        for g in range(SIZE[kind]):
                            n = first[(kind, c)] + g
                            bank = banks[:, n % BANKS, :]
                            if isinstance(b, int) and n == HIS:
                                pe.wait_ge(weights_ready, 2)
                            need = PER * b + (n + 1 - BANKS)
                            if positive(need):
                                pe.wait_ge(bank_free, need)
                            if kind == "KV" and g < HIS:
                                last = pair_product(pe, bank, weight(1, slice(g * P, (g + 1) * P)),
                                                    lambda k: (ctx_h[:, c % 2, k, :], ctx_l[:, c % 2, k, :]))
                            elif kind == "KV":
                                rows = slice((g - HIS) * P, (g - HIS + 1) * P)
                                last = pair_product(pe, bank,
                                                    lambda k: (ctx_h[:, c % 2, k, rows], ctx_l[:, c % 2, k, rows]),
                                                    weight(2, slice(0, D)))
                            elif kind == "Q":
                                last = pair_product(pe, bank, weight(0, slice(g * P, (g + 1) * P)),
                                                    lambda k: (xT_h[:, k, :], xT_l[:, k, :]))
                            else:
                                for s in range(ST):
                                    last = pe.transpose(bank[:, s * P:(s + 1) * P], xn[:, s, g * P:(g + 1) * P],
                                                        ident[:])
                            last.then_inc(bank_filled, 1)

                pe.wait_ge(weights_ready, 1)
                pe.wait_ge(ident_ready, 1)
                batch(0)
                with pe.Fori(1, B) as b:
                    batch(b)


def load_rows(sp, i, c, ahead, x, s_heads, s_den):
    x_f, heads, den, rows_loaded = ahead
    sp.dma_start(x_f[:, c % 2], x[bass.ds(i * SQ + c * N, N), :].rearrange("(s p) d -> p s d", p=P)
                 ).then_inc(rows_loaded[c % 2], 16)
    start = c // 2 * GROUPS * QC
    sp.dma_start(heads[:, c % 2], s_heads[bass.ds(i * (GROUPS * QC * P) + start * P, GROUPS * QC * P), :].rearrange(
        "(g c p) t -> c p g t", g=GROUPS, c=QC)[c % 2]).then_inc(rows_loaded[c % 2], 16)
    sp.dma_start(den[0:H, c % 2, :], s_den[bass.ds(i * H + (c % 2 * (UNITS * HG) + c // 2 * H), H), :]
                 ).then_inc(rows_loaded[c % 2], 16)


def attend(nc, ident, banks, s_K, s_Q, s_V, s_mask, s_ones, s_heads, s_den, x, ahead,
           w1, w2, w1_h, w1_l, w2_h, w2_l):
    HI0, HI1, LO, MASK_ROW, ONE_ROW, ROWS = 0, W, 2 * W, 3 * W, 3 * W + 1, 3 * W + 2
    STEPS = 2 * QC
    TURNS = UNITS // 2
    PAIRS = JT // 2
    PER = STEPS * PAIRS
    QUADS = PER // 2
    ITEMS = HG * ST * CC
    SLOTS = ITEMS + 1
    TURN_AT = 2
    AHEAD = 2 * PAIRS
    SHARE_AT = 2
    SCORES = 2 * HG
    SCORE_BANKS, SLOT_BANK, SLOT_BANKS, O_BANK, DEN_BANK = 3, 3, 3, 6, 7
    SLOTS_AFTER = ((1, 0, 1, 0, 2, 1, 0, 1, 0, 1, 0), (1, 0, 1, 0, 2, 1, 0, 1, 0, 2, 1))
    STACK_DMAS = 3 + 3 * QC + 1
    with ExitStack() as ctx:
        def sb(name, shape, dt):
            return ctx.enter_context(nc.sbuf_tensor(name, shape, dt))

        def sem(name):
            return ctx.enter_context(nc.semaphore(name))

        K = sb("K_stack", [ROWS, 2, HG, SKV], F16)
        Q = sb("Q_stack", [ROWS, 2, QC, HG * N], F16)
        V = ahead[1][:].rearrange("p b g t -> p b (g t)").rearrange("p b (j e) -> p b j e", e=P)
        probs = sb("probs", [P, 2, 2, HG, N], F32)
        quad_sum = sb("quad_sum", [P, 2, HG, N], F32)
        ones = sb("ones", [P, W], F32)
        maxima = sb("maxima", [P, 2, ITEMS], F32)
        neg_max = sb("neg_max", [P, 2, P], F32)
        shift = sb("shift", [P, 2, P], F16)
        o_raw = sb("o_raw", [P, 2, N], F32)
        den = sb("den", [P, 2, N], F32)
        w_stage = ahead[0][:].rearrange("p b s d -> p b (s d)")

        consts_ready = sem("b_consts_ready")
        ones_loaded = sem("ones_loaded")
        stacks_loaded = [sem(f"stacks_loaded{i}") for i in range(2)]
        V_loaded = [sem(f"V_loaded{i}") for i in range(2)]
        slot_filled = sem("slot_filled")
        slot_free = sem("slot_free")
        neg_max_ready = sem("neg_max_ready")
        shift_loaded = [sem(f"shift_loaded{i}") for i in range(2)]
        scores_ready = sem("scores_ready")
        exp_done = sem("exp_done")
        pv_done = sem("pv_done")
        pool_summed = sem("pool_summed")
        dve_summed = sem("dve_summed")
        dve_third = sem("dve_third")
        den_done = sem("den_done")
        o_copied = sem("o_copied")
        den_copied = sem("den_copied")
        heads_stored = [sem(f"heads_stored{i}") for i in range(2)]
        w_loaded = [sem(f"w_loaded{i}") for i in range(2)]
        w_hi_done = sem("w_hi_done")
        w_lo_done = sem("w_lo_done")

        RT = DFF // D
        pieces = [(w1[k * P:(k + 1) * P, :], w1_h[:, k, :], w1_l[:, k, :]) for k in range(KT)]
        pieces += [(w2[k * RT * P:(k + 1) * RT * P, :].rearrange("(f p) d -> p f d", p=P),
                    w2_h[:, RT * k:RT * (k + 1), :].rearrange("p f d -> p (f d)"),
                    w2_l[:, RT * k:RT * (k + 1), :].rearrange("p f d -> p (f d)")) for k in range(FT // RT)]

        def slot_runs(s, p):
            assert SLOTS == 8 * PAIRS + 1
            start = SLOTS * (s + 1) + AHEAD + 8 * p + (p > 0 and p % 2 == 0)
            return [divmod(n, SLOTS) for n in range(start, start + (8 if p == 0 else 7 if p % 2 == 0 else 9))]

        def slots_of(s, p, last):
            return [(t, k) for t, k in slot_runs(s, p) if not last or t < STEPS or (t == STEPS and k == TURN_AT)]

        def item_of(k):
            item = k if k < TURN_AT else k - 1
            return item // (ST * CC), item // CC % ST, item % CC

        def first(i):
            return isinstance(i, int) and i == 0

        def is_tail(i, g):
            return isinstance(i, int) and i == TURNS - 1 and g >= QUADS - PAIRS // 2

        def pool_heads(i, g):
            return HG // 2 if is_tail(i, g) else HG - 1

        def slot_bank(t, k):
            return banks[:, SLOT_BANK + (SLOTS * t + k) % (SLOTS * STEPS) % SLOT_BANKS, :]

        def turns(eng, body):
            body(0, False)
            with eng.Fori(1, TURNS - 1) as i:
                body(i, False)
            body(TURNS - 1, True)

        OPENING = [(0, k) for k in range(SLOTS)] + [(1, k) for k in range(AHEAD)]

        def slot_number(i, t, k):
            skipped = TURN_AT if isinstance(i, int) and i == TURNS - 1 and t == STEPS else 0
            return SLOTS * STEPS * i + (SLOTS * t + k - skipped)

        with nc.Block() as block:
            @block.sync
            def _(sp):
                def load_unit(i, u):
                    need = PER * i + (u - 1) * (PER // 2)
                    if positive(need):
                        sp.wait_ge(pv_done, need)
                    buf, got = u % 2, stacks_loaded[u % 2]
                    rows = bass.ds(i * (2 * P) + u * P, P)
                    for at, s_k in ((HI0, s_K[0]), (HI1, s_K[0]), (LO, s_K[1])):
                        sp.dma_start(K[at:at + W, buf], s_k[rows, :].rearrange("(h w) t -> w h t", w=W)).then_inc(got, 16)
                    for at, s_q in ((HI0, s_Q[0]), (HI1, s_Q[1]), (LO, s_Q[0])):
                        for c in range(QC):
                            sp.dma_start(Q[at:at + W, buf, c, :].rearrange("w (h t) -> w h t", h=HG),
                                         s_q[rows, c * N:(c + 1) * N].rearrange("(h w) t -> w h t", w=W)
                                         ).then_inc(got, 16)
                    sp.dma_start(K[MASK_ROW:MASK_ROW + 1, buf], s_mask[bass.ds(i * 2 + u, 1), :].unsqueeze(1)
                                 .to_broadcast([1, HG, SKV])).then_inc(got, 16)
                    half = SKV // 2
                    for k in range(2):
                        sp.dma_start(V[:, buf, k * JT // 2:(k + 1) * JT // 2, :],
                                     s_V[bass.ds(i * (2 * SKV) + (u * SKV + k * half), half), :].rearrange(
                                         "(j p) e -> p j e", p=P)).then_inc(V_loaded[buf], 16)

                def load_shift(i, t):
                    sp.wait_ge(slot_free, slot_number(i, t + 1, TURN_AT) + 1)
                    buf, c = t // QC % 2, t % QC
                    sp.dma_start(Q[ONE_ROW:ONE_ROW + 1, buf, c, :], shift[0:HG * ST, t % 2, :]).then_inc(shift_loaded[t % 2], 16)

                def store_heads(i, s):
                    sp.wait_ge(o_copied, STEPS * i + (s + 1))
                    sp.dma_start(s_heads[bass.ds(i * (STEPS * P) + s * P, P), :], o_raw[:, s % 2, :]
                                 ).then_inc(heads_stored[s % 2], 16)
                    sp.wait_ge(den_copied, STEPS * i + (s + 1))
                    sp.dma_start(s_den[bass.ds(i * (2 * HG) + (s % QC * (UNITS * HG) + s // QC * HG), HG), :], den[0:P:W, s % 2, :]
                                 ).then_inc(heads_stored[s % 2], 16)

                def turn(i, last):
                    load_unit(i, 1)
                    if not first(i):
                        store_heads(i, -1)
                    load_shift(i, 1)
                    store_heads(i, 0)
                    load_shift(i, 2)
                    if not last:
                        load_unit(i, 2)
                    else:
                        sp.wait_ge(w_lo_done, len(pieces))
                        sp.wait_ge(consts_ready, 3)
                        sp.wait_ge(pv_done, PER * i + PER // 2)
                        sp.wait_ge(heads_stored[0], 32 * (STEPS // 2 * i + 1))
                        sp.wait_ge(heads_stored[1], 32 * (STEPS // 2 * i))
                        load_rows(sp, 0, 0, ahead, x, s_heads, s_den)
                    store_heads(i, 1)
                    load_shift(i, 3)
                    store_heads(i, 2)
                    if not last:
                        load_shift(i, 4)

                ones_row = s_ones.rearrange("(o u) t -> o (u t)", o=1)
                load_unit(0, 0)
                for buf in range(2):
                    sp.dma_start(K[ONE_ROW:ONE_ROW + 1, buf].rearrange("o h t -> o (h t)"), ones_row
                                 ).then_inc(ones_loaded, 16)
                    sp.dma_start(Q[MASK_ROW:MASK_ROW + 1, buf].rearrange("o c t -> o (c t)"),
                                 ones_row[:, 0:QC * HG * N]).then_inc(ones_loaded, 16)
                for n, (src, _, _) in enumerate(pieces):
                    need = n - 1
                    if positive(need):
                        sp.wait_ge(w_lo_done, need)
                    to = w_stage[:, n % 2, :] if n < KT else w_stage[:, n % 2, :].rearrange("p (f d) -> p f d", f=RT)
                    sp.dma_start(to, src).then_inc(w_loaded[n % 2], 16)
                load_shift(0, 0)
                turns(sp, turn)
                store_heads(TURNS - 1, STEPS - 1)
                for k in range(2):
                    sp.wait_ge(heads_stored[k], 32 * STEPS * TURNS // 2)

            @block.gpsimd
            def _(pool):
                def turn(i, last):
                    for g in range(QUADS):
                        Q4, total, own = QUADS * i + g, quad_sum[:, g % 2], pool_heads(i, g)
                        third = own if is_tail(i, g) else HG
                        need = Q4 - 1
                        if positive(need):
                            pool.wait_ge(den_done, need)
                        pool.wait_ge(exp_done, SCORES * (2 * Q4 + 1))
                        pool.tensor_tensor(total[:, 0:own], probs[:, 0, 0, 0:own], probs[:, 0, 1, 0:own], ALU.add
                                           ).then_inc(pool_summed, 1)
                        pool.wait_ge(exp_done, SCORES * (2 * Q4 + 1) + HG)
                        if third == HG:
                            pool.wait_ge(dve_summed, 2 * Q4 + 1)
                        pool.wait_ge(pool_summed, 3 * Q4 + 1)
                        pool.tensor_tensor(total[:, 0:third], total[:, 0:third], probs[:, 1, 0, 0:third], ALU.add
                                           ).then_inc(pool_summed, 1)
                        pool.wait_ge(exp_done, SCORES * (2 * Q4 + 2))
                        pool.wait_ge(pool_summed, 3 * Q4 + 2)
                        pool.tensor_tensor(total[:, 0:own], total[:, 0:own], probs[:, 1, 1, 0:own], ALU.add
                                           ).then_inc(pool_summed, 1)

                pool.memset(neg_max[:], 0.0).then_inc(consts_ready, 1)
                pool.memset(ahead[2][:], 0.0).then_inc(consts_ready, 1)
                for n, (_, hi, lo) in enumerate(pieces):
                    pool.wait_ge(w_hi_done, n + 1)
                    pool.tensor_tensor(lo, w_stage[:, n % 2], hi, ALU.subtract).then_inc(w_lo_done, 1)
                turns(pool, turn)

            @block.scalar
            def _(act):
                def copy_out(i, s, done, value, bank, to, copied):
                    act.wait_ge(done, value)
                    need = 32 * (STEPS // 2 * i + s // 2)
                    if positive(need):
                        act.wait_ge(heads_stored[s % 2], need)
                    act.activation(to[:, s % 2, :], banks[:, bank, :], ACT.Copy).then_inc(copied, 1)

                def copy_o(i, s):
                    copy_out(i, s, pv_done, PER * i + PAIRS * (s + 1), O_BANK, o_raw, o_copied)

                def copy_den(i, s):
                    copy_out(i, s, den_done, QUADS * i + PAIRS // 2 * (s + 1), DEN_BANK, den, den_copied)

                def turn(i, last):
                    for t in range(PER):
                        G = PER * i + t
                        need = G - 1
                        if positive(need):
                            act.wait_ge(pv_done, need)
                        Q4 = QUADS * i + t // 2
                        need = 3 * Q4 - 2 * (1 - t % 2)
                        if positive(need):
                            act.wait_ge(pool_summed, need)
                        need = 2 * Q4 - (1 - t % 2)
                        if positive(need):
                            act.wait_ge(dve_summed, need)
                        for q in range(SCORES):
                            act.wait_ge(scores_ready, SCORES * G + (q + 1))
                            act.activation(probs[:, t % 2, q // HG, q % HG, :], banks[:, q % SCORE_BANKS, :], ACT.Exp
                                           ).then_inc(exp_done, 1)
                        if t % PAIRS == 0 and not (first(i) and t < PAIRS):
                            copy_o(i, t // PAIRS - 1)
                        if t % PAIRS == 1 and not (first(i) and t < PAIRS):
                            copy_den(i, t // PAIRS - 1)

                for n, (_, hi, _) in enumerate(pieces):
                    act.wait_ge(w_loaded[n % 2], 16 * (n // 2 + 1))
                    act.activation(hi, w_stage[:, n % 2], ACT.Copy).then_inc(w_hi_done, 1)
                turns(act, turn)
                copy_o(TURNS - 1, STEPS - 1)
                copy_den(TURNS - 1, STEPS - 1)

            @block.vector
            def _(dve):
                def slot(i, t, k):
                    n = slot_number(i, t, k)
                    par = t % 2
                    dve.wait_ge(slot_filled, n + 1)
                    bank = slot_bank(t, k)
                    if k == TURN_AT:
                        need = 16 * (STEPS // 2 * i + (t - 1) // 2)
                        if positive(need):
                            dve.wait_ge(shift_loaded[1 - par], need)
                        dve.tensor_copy(shift[0:HG * ST, 1 - par, :], bank[0:HG * ST, 0:P]).then_inc(slot_free, 1)
                        return
                    item = k if k < TURN_AT else k - 1
                    dve.tensor_reduce(maxima[:, par, item:item + 1], bank, AX_X, ALU.max).then_inc(slot_free, 1)
                    if k == SLOTS - 1:
                        dve.wait_ge(slot_free, n + 1)
                        dve.tensor_reduce(neg_max[:, par, 0:HG * ST],
                                          maxima[:, par, :].rearrange("p (r c) -> p r c", c=CC), AX_X, ALU.max,
                                          negate=True).then_inc(neg_max_ready, 1)

                def add_last_head(i, t):
                    if t < 0 and first(i):
                        return
                    Q4, own = QUADS * i + t // 2, slice(pool_heads(i, t // 2), HG)
                    total = quad_sum[:, t // 2 % 2, own, :]
                    dve.wait_ge(exp_done, SCORES * (PER * i + (t + 1)))
                    if t % 2 == 0:
                        need = Q4 - 1
                        if positive(need):
                            dve.wait_ge(den_done, need)
                        dve.tensor_tensor(total, probs[:, 0, 0, own, :], probs[:, 0, 1, own, :], ALU.add
                                          ).then_inc(dve_summed, 1)
                    else:
                        if is_tail(i, t // 2):
                            dve.wait_ge(dve_summed, 2 * Q4 + 1)
                            dve.tensor_tensor(total, total, probs[:, 1, 0, own, :], ALU.add).then_inc(dve_third, 1)
                            dve.wait_ge(dve_third, t // 2 - (QUADS - PAIRS // 2) + 1)
                        else:
                            dve.wait_ge(pool_summed, 3 * Q4 + 2)
                        dve.tensor_tensor(total, total, probs[:, 1, 1, own, :], ALU.add).then_inc(dve_summed, 1)

                def turn(i, last):
                    for t in range(PER):
                        for n, when in enumerate(slots_of(t // PAIRS, t % PAIRS, last)):
                            if n == SHARE_AT:
                                add_last_head(i, t - 1)
                            slot(i, *when)
                        if len(slots_of(t // PAIRS, t % PAIRS, last)) <= SHARE_AT:
                            add_last_head(i, t - 1)

                dve.memset(ones[:], 1.0).then_inc(consts_ready, 1)
                dve.wait_ge(consts_ready, 3)
                for when in OPENING:
                    slot(0, *when)
                turns(dve, turn)
                add_last_head(TURNS - 1, PER - 1)

            @block.tensor
            def _(pe):
                def slot(i, t, k):
                    n = slot_number(i, t, k)
                    need = n - 2 + ((SLOTS * t + k) % (SLOTS * STEPS) < SLOT_BANKS - 1)
                    if positive(need):
                        pe.wait_ge(slot_free, need)
                    bank = slot_bank(t, k)
                    if k == TURN_AT:
                        need = STEPS * i + t
                        if positive(need):
                            pe.wait_ge(neg_max_ready, need)
                        pe.transpose(bank[:, 0:P], neg_max[:, 1 - t % 2, :], ident[:]).then_inc(slot_filled, 1)
                        return
                    buf, c = t // QC % 2, t % QC
                    if k == 0 and t % QC == 0:
                        pe.wait_ge(stacks_loaded[buf], 16 * STACK_DMAS * (i + t // (2 * QC) + 1))
                    h, tile, chunk = item_of(k)
                    pe.matmul(bank, Q[0:ONE_ROW, buf, c, h * N + tile * P:h * N + (tile + 1) * P],
                              K[0:ONE_ROW, buf, h, chunk * N:(chunk + 1) * N], start=True, stop=True
                              ).then_inc(slot_filled, 1)

                def scores(i, t, q):
                    s, j, h = t // PAIRS, 2 * (t % PAIRS) + q // HG, q % HG
                    buf, c = s // QC, s % QC
                    if t % PAIRS == 0 and q == 0:
                        pe.wait_ge(shift_loaded[s % 2], 16 * (STEPS // 2 * i + (s // 2 + 1)))
                    need = SCORES * (PER * i + t) + (q - 2 + (q < SCORE_BANKS - 1))
                    if positive(need):
                        pe.wait_ge(exp_done, need)
                    pe.matmul(banks[:, q % SCORE_BANKS, :], K[0:ROWS, buf, h, j * P:(j + 1) * P],
                              Q[0:ROWS, buf, c, h * N:(h + 1) * N], start=True, stop=True).then_inc(scores_ready, 1)

                def values(i, t, jj):
                    if t < 0 and first(i):
                        return
                    s, p = t // PAIRS, t % PAIRS
                    if jj == 0:
                        pe.wait_ge(exp_done, SCORES * (PER * i + (t + 1)))
                        if p == 0:
                            if s % QC == 0:
                                pe.wait_ge(V_loaded[s // QC], 32 * (i + 1))
                            need = STEPS * i + s
                            if positive(need):
                                pe.wait_ge(o_copied, need)
                    for h in range(HG):
                        last = pe.matmul(banks[h * W:(h + 1) * W, O_BANK, :], V[:, s // QC % 2, 2 * p + jj, h * W:(h + 1) * W],
                                         probs[:, t % 2, jj, h, :], start=(p == 0 and jj == 0),
                                         stop=(p == PAIRS - 1 and jj == 1))
                    if jj == 1:
                        last.then_inc(pv_done, 1)

                def denominators(i, g):
                    if g < 0 and first(i):
                        return
                    Q4, part = QUADS * i + g, g % (PAIRS // 2)
                    pe.wait_ge(pool_summed, 3 * Q4 + 3)
                    pe.wait_ge(dve_summed, 2 * Q4 + 2)
                    if part == 0:
                        need = STEPS * i + g // (PAIRS // 2)
                        if positive(need):
                            pe.wait_ge(den_copied, need)
                    for h in range(HG):
                        last = pe.matmul(banks[h * W:(h + 1) * W, DEN_BANK, :], ones[:], quad_sum[:, g % 2, h, :],
                                         start=(part == 0), stop=(part == PAIRS // 2 - 1))
                    last.then_inc(den_done, 1)

                def turn(i, last):
                    for t in range(PER):
                        todo = slots_of(t // PAIRS, t % PAIRS, last)
                        counts = SLOTS_AFTER[t % 2]

                        def slots_after(n):
                            start = sum(counts[:n])
                            for when in todo[start:start + counts[n] if n < len(counts) - 1 else None]:
                                slot(i, *when)

                        for jj in range(2):
                            for h in range(HG):
                                scores(i, t, jj * HG + h)
                                slots_after(jj * (HG + 1) + h)
                            values(i, t - 1, jj)
                            slots_after(jj * (HG + 1) + HG)
                        if t % 2:
                            denominators(i, t // 2 - 1)
                        slots_after(2 * (HG + 1))

                pe.wait_ge(consts_ready, 3)
                pe.wait_ge(ones_loaded, 16 * 4)
                for when in OPENING:
                    slot(0, *when)
                turns(pe, turn)
                values(TURNS - 1, PER - 1, 0)
                values(TURNS - 1, PER - 1, 1)
                denominators(TURNS - 1, QUADS - 1)


def ffn(nc, ident, banks, x, s_heads, s_den, ahead, g_attn, g_ffn, m1, m2, mb, b2, w1_h, w1_l, w2_h, w2_l, out):
    ITEMS = ST * (DFF // N)
    QT = DFF // N
    CHUNKS = 2
    PER = CHUNKS * ITEMS
    AT_X1 = 1
    AT_NT = AT_X1 + ST
    AT_LR = AT_NT + KT
    PREPS = AT_LR + 1
    GB = N // D2
    RT = N // P
    BIAS_HI, BIAS_LO = 0, W
    with ExitStack() as ctx:
        def sb(name, shape, dt):
            return ctx.enter_context(nc.sbuf_tensor(name, shape, dt))

        def sem(name):
            return ctx.enter_context(nc.semaphore(name))

        scale = sb("scale", [P, 2, ST, H], F32)
        x1 = sb("x1", [P, 2, ST, D], F32)
        x_f, heads, den, rows_loaded = ahead
        xn = sb("c_xn", [P, ST, D], F32)
        xT_h = sb("c_xT_h", [P, 2, KT, N], F16)
        xT_l = sb("c_xT_l", [P, 2, KT, N], F16)
        lr_h = sb("lr_h", [P, 2, N], F16)
        lr_l = sb("lr_l", [P, 2, N], F16)
        peak = sb("peak", [P, 2, GB], F32)
        is_peak = sb("is_peak", [P, 2, N], F32)
        goes_on = sb("goes_on", [P, N], F32)
        count = sb("count", [P, 2, N], F32)
        relu = sb("relu", [P, 2, N], F32)
        act_f = sb("act_f", [P, 2, N], F32)
        aT_h = sb("aT_h", [P, 2, RT, P], F16)
        aT_l = sb("aT_l", [P, 2, RT, P], F16)
        result = sb("result", [P, 2, D], F32)
        gate = sb("gate", [P, 2, 2], F32)
        b2_f = sb("b2_f", [P, D], F32)
        b2_g = sb("b2_g", [P, D], F32)
        m1_f = sb("m1_f", [P, KT, 2 * DL], F32)
        m1_h = sb("m1_h", [P, KT, 2 * DL], F16)
        m1_l = sb("m1_l", [P, KT, 2 * DL], F16)
        m2_f = sb("m2_f", [P, DFF], F32)
        mb_f = sb("mb_f", [2 * W, DFF], F32)
        mb_h = sb("mb_h", [2 * W, DFF], F16)
        m2_1 = sb("m2_1", [P, DFF], F16)
        m2_2 = sb("m2_2", [P, DFF], F16)
        stats = sb("c_stats", [P, ST, 6], F32)
        moments = sb("c_moments", [P, 3, ST], F32)
        small = sb("c_small", [P, 5, ST], F32)

        gates_loaded = sem("gates_loaded")
        gates_ready = sem("gates_ready")
        consts_loaded = sem("c_consts_loaded")
        zeros_ready = sem("zeros_ready")
        consts_hi = sem("c_consts_hi")
        consts_ready = sem("c_consts_ready")
        bias_hi = sem("bias_hi")
        bias_ready = sem("bias_ready")
        b2_ready = sem("b2_ready")
        prep_filled = sem("prep_filled")
        prep_hi = sem("prep_hi")
        prep_free = sem("prep_free")
        ln_step = sem("c_ln_step")
        sqrt_done = sem("c_sqrt_done")
        logits_filled = sem("logits_filled")
        mid_filled = sem("mid_filled")
        aT_filled = sem("aT_filled")
        w2_done = sem("w2_done")
        peak_done = sem("peak_done")
        is_peak_done = sem("is_peak_done")
        count_done = sem("count_done")
        relu_done = sem("relu_done")
        act_done = sem("act_done")
        aT_hi_done = sem("aT_hi_done")
        aT_lo_done = sem("aT_lo_done")
        inverted = sem("inverted")
        x1_done = sem("x1_done")
        biased = sem("biased")
        result_ready = sem("result_ready")
        result_stored = [sem(f"result_stored{i}") for i in range(2)]

        LOADS = 3
        PREP_BANK, Y_BANK = 7, 6

        def prep_at(t):
            return {0: [0, 1], 1: [2], 2: [3], 3: [4], 9: [5], 10: [6], 11: [7], 12: [8], 14: [9]}.get(t, [])

        STATS_AT, SQRT_AT, SCALE_AT, APPLY_AT = 2, 5, 6, (7, 8)

        def prep_bank(i, c, n):
            return banks[:, n % BANKS if isinstance(i, int) and i == c == 0 else PREP_BANK, :]

        def turns(eng, body):
            body(0, False)
            with eng.Fori(1, B - 1) as i:
                body(i, False)
            body(B - 1, True)

        with nc.Block() as block:
            @block.sync
            def _(sp):
                def load_next(i, c):
                    sp.wait_ge(x1_done, ST * (2 * i + (c - 1)))
                    load_rows(sp, i, c, ahead, x, s_heads, s_den)

                def store(i, c, s):
                    n = ST * c + s
                    sp.wait_ge(result_ready, 2 * ST * i + (n + 1))
                    sp.dma_start(out[bass.ds(i * SQ + n * P, P), :], result[:, n % 2, :]
                                 ).then_inc(result_stored[n % 2], 16)

                def turn(i, last):
                    for c in range(CHUNKS):
                        for s in range(ST):
                            store(i, c, s)
                            if s == 0 and not last:
                                load_next(i, c + 2)

                for n, g in enumerate((g_attn, g_ffn)):
                    sp.dma_start(gate[:, 0, n:n + 1], g.partition_broadcast(P)).then_inc(gates_loaded, 16)
                for at in (0, DL):
                    sp.dma_start(m2_f[at:at + DL, :], m2).then_inc(consts_loaded, 16)
                for at in (BIAS_HI, BIAS_LO):
                    sp.dma_start(mb_f[at:at + 1, :], mb).then_inc(consts_loaded, 16)
                for at in (0, DL):
                    sp.dma_start(m1_f[:, :, at:at + DL], m1.rearrange("(k p) l -> p k l", p=P)
                                 ).then_inc(consts_loaded, 16)
                sp.dma_start(b2_f[:], b2.partition_broadcast(P)).then_inc(consts_loaded, 16)
                load_rows(sp, 0, 1, ahead, x, s_heads, s_den)
                turns(sp, turn)
                for k in range(2):
                    sp.wait_ge(result_stored[k], 16 * (SQ // P * B // 2))

            @block.gpsimd
            def _(pool):
                pool.memset(m2_2[0:DL, :], 0.0).then_inc(zeros_ready, 1)
                pool.memset(lr_l[:], 1.0).then_inc(zeros_ready, 1)
                pool.memset(goes_on[:], 1.0).then_inc(zeros_ready, 1)
                pool.wait_ge(zeros_ready, 3)
                pool.memset(goes_on[:].rearrange("p (g d) -> p g d", d=D2)[:, :, 0:1], 0.0).then_inc(zeros_ready, 1)

                def add(i, c, s):
                    need = ST * (2 * i + (c - 1))
                    if positive(need):
                        pool.wait_ge(result_ready, need)
                    pool.wait_ge(rows_loaded[c % 2], 16 * LOADS * (i + (c // 2 + 1)))
                    pool.wait_ge(prep_free, PREPS * (2 * i + c) + (AT_X1 + s + 1))
                    pool.tensor_tensor(x1[:, c % 2, s, :], xn[:, s, :], x_f[:, c % 2, s, :], ALU.add
                                       ).then_inc(x1_done, 1)

                def bias(i, c):
                    pool.wait_ge(ln_step, LN_STEPS * (2 * i + (c + 1)))
                    pool.wait_ge(x1_done, ST * (2 * i + (c + 1)))
                    pool.tensor_tensor(x1[:, c % 2], x1[:, c % 2], b2_g[:].unsqueeze(1).to_broadcast([P, ST, D]), ALU.add
                                       ).then_inc(biased, 1)

                def turn(i, last):
                    for c in range(CHUNKS):
                        if last and c == 1:
                            continue
                        for s in range(ST):
                            add(i, c + 1, s)
                        bias(i, c + 1)

                for s in range(ST):
                    add(0, 0, s)
                pool.wait_ge(bias_hi, 2)
                pool.tensor_tensor(m2_2[BIAS_LO:BIAS_LO + 1, :], mb_f[BIAS_LO:BIAS_LO + 1, :],
                                   mb_h[BIAS_LO:BIAS_LO + 1, :], ALU.subtract).then_inc(bias_ready, 1)
                pool.wait_ge(bias_ready, 1)
                pool.wait_ge(b2_ready, 1)
                bias(0, 0)
                turns(pool, turn)

            @block.scalar
            def _(act):
                def prep(i, c, n):
                    C = 2 * i + c
                    bank = prep_bank(i, c, n)
                    if n < AT_NT:
                        return
                    act.wait_ge(prep_filled, PREPS * C + (n + 1))
                    to = xT_h[:, c % 2, n - AT_NT, :] if n < AT_LR else lr_h[:, c % 2, :]
                    act.activation(to, bank, ACT.Copy).then_inc(prep_hi, 1)

                def item(i, u):
                    U = PER * i + u
                    if isinstance(U, int) and U < 0:
                        return
                    act.wait_ge(aT_filled, U + 1)
                    need = U - 1
                    if positive(need):
                        act.wait_ge(w2_done, need)
                    act.activation(aT_h[:, u % 2].rearrange("p f t -> p (f t)"), banks[:, 4 + u % 2, :], ACT.Copy
                                   ).then_inc(aT_hi_done, 1)

                def turn(i, last):
                    for u in range(PER):
                        item(i, u - 1)
                        c, t = divmod(u, ITEMS)
                        if last and c == 1:
                            continue
                        for n in prep_at(t):
                            prep(i, c + 1, n)
                        if t == SQRT_AT:
                            scalar_layer_norm(act, 2 * i + (c + 1), small, sqrt_done, ln_step)

                act.wait_ge(gates_loaded, 16 * 2)
                act.activation(gate[:, 1, :], gate[:, 0, :], ACT.Tanh).then_inc(gates_ready, 1)
                act.wait_ge(consts_loaded, 16 * 7)
                act.activation(m1_h[:], m1_f[:], ACT.Copy).then_inc(consts_hi, 1)
                act.activation(m2_1[0:DL, :], m2_f[0:DL, :], ACT.Copy).then_inc(consts_hi, 1)
                act.activation(m2_2[DL:2 * DL, :], m2_f[DL:2 * DL, :], ACT.Copy).then_inc(consts_hi, 1)
                scalar_layer_norm(act, 0, small, sqrt_done, ln_step)
                act.activation(mb_h[BIAS_LO:BIAS_LO + 1, :], mb_f[BIAS_LO:BIAS_LO + 1, :], ACT.Copy).then_inc(bias_hi, 1)
                act.wait_ge(zeros_ready, 4)
                act.activation(m2_2[BIAS_HI:BIAS_HI + 1, :], mb_f[BIAS_HI:BIAS_HI + 1, :], ACT.Copy).then_inc(bias_hi, 1)
                for n in range(PREPS):
                    prep(0, 0, n)
                turns(act, turn)
                item(0, PER * B - 1)

            @block.vector
            def _(dve):
                def prep(i, c, n):
                    C = 2 * i + c
                    bank = prep_bank(i, c, n)
                    if n < AT_NT:
                        dve.wait_ge(prep_filled, PREPS * C + (n + 1))
                    if n == 0:
                        dve.reciprocal(scale[:, 0], bank.rearrange("p (s c) -> p s c", c=P)[:, :, 0:H]).then_inc(inverted, 1)
                        dve.wait_ge(inverted, C + 1)
                        ins = dve.tensor_scalar(scale[:, 1].rearrange("p s h -> p (s h)"),
                                                scale[:, 0].rearrange("p s h -> p (s h)"), gate[:, 1, 0:1], None,
                                                ALU.mult)
                    elif n < AT_NT:
                        if n == AT_X1:
                            dve.wait_ge(prep_free, PREPS * C + AT_X1)
                        s = n - AT_X1
                        dve.tensor_tensor(xn[:, s, :].rearrange("p (h w) -> p h w", w=W),
                                          bank.rearrange("p (h w) -> p h w", w=W),
                                          scale[:, 1, s, :].unsqueeze(2).to_broadcast([P, H, W]), ALU.mult
                                          ).then_inc(prep_free, 1)
                        return
                    else:
                        dve.wait_ge(prep_hi, (KT + 1) * C + (n - AT_NT + 1))
                        if n < AT_LR:
                            ins = dve.tensor_tensor(xT_l[:, c % 2, n - AT_NT, :], bank, xT_h[:, c % 2, n - AT_NT, :],
                                                    ALU.subtract)
                        else:
                            ins = dve.tensor_tensor(lr_l[DL:2 * DL, c % 2, :], bank[DL:2 * DL, :],
                                                    lr_h[DL:2 * DL, c % 2, :], ALU.subtract)
                    ins.then_inc(prep_free, 1)

                def norm_at(i, c, t):
                    n, rows = 2 * i + c, x1[:, c % 2]
                    s = t - STATS_AT
                    if s in range(ST):
                        dve.wait_ge(x1_done, ST * n + (s + 1))
                        ins = dve.bn_stats(stats[:, s, :], rows[:, s, :])
                        if s == ST - 1:
                            ins.then_inc(ln_step, 1)
                    if t == SQRT_AT:
                        norm_statistics(dve, n, moments, stats, small, ln_step)
                    if t == SCALE_AT:
                        norm_scale(dve, n, small, sqrt_done, ln_step)
                    if t in APPLY_AT:
                        half = ST // 2 * APPLY_AT.index(t)
                        norm_apply(dve, n, rows, xn, moments, small, ln_step, range(half, half + ST // 2))

                def lo_part(i, u):
                    U = PER * i + u
                    if isinstance(U, int) and U < 0:
                        return
                    dve.wait_ge(aT_hi_done, U + 1)
                    dve.tensor_tensor(aT_l[:, u % 2].rearrange("p f t -> p (f t)"), banks[:, 4 + u % 2, :],
                                      aT_h[:, u % 2].rearrange("p f t -> p (f t)"), ALU.subtract
                                      ).then_inc(aT_lo_done, 1)

                def finish(i, u):
                    U = PER * i + u
                    if (isinstance(U, int) and U < 0) or u % QT != QT - 1:
                        return
                    r = u // QT % (2 * ST)
                    dve.wait_ge(w2_done, U + 1)
                    dve.wait_ge(biased, 2 * i + (u // (QT * ST) + 1))
                    need = 16 * (ST * i + u // QT // 2)
                    if positive(need):
                        dve.wait_ge(result_stored[r % 2], need)
                    dve.scalar_tensor_tensor(result[:, r % 2, :], banks[:, Y_BANK, :], gate[:, 1, 1:2],
                                             x1[:, r // ST, r % ST, :], ALU.mult, ALU.add).then_inc(result_ready, 1)

                def item(i, u):
                    U = PER * i + u
                    par = u % 2
                    logits = banks[:, par, :].rearrange("p (g d) -> p g d", d=D2)
                    dve.wait_ge(logits_filled, U + 1)
                    dve.tensor_reduce(peak[:, par, :], logits, AX_X, ALU.max).then_inc(peak_done, 1)
                    dve.wait_ge(peak_done, U + 1)
                    dve.tensor_tensor(is_peak[:, par, :].rearrange("p (g d) -> p g d", d=D2), logits,
                                      peak[:, par, :].unsqueeze(2).to_broadcast([P, GB, D2]), ALU.is_equal
                                      ).then_inc(is_peak_done, 1)
                    dve.wait_ge(is_peak_done, U + 1)
                    dve.tensor_tensor_scan(count[:, par, :], goes_on[:], is_peak[:, par, :], 0.0, ALU.mult, ALU.add
                                           ).then_inc(count_done, 1)
                    dve.wait_ge(mid_filled, U + 1)
                    dve.scalar_tensor_tensor(relu[:, par, :], banks[:, 2 + par, :], 0.0, is_peak[:, par, :],
                                             ALU.max, ALU.mult).then_inc(relu_done, 1)
                    lo_part(i, u - 1)
                    dve.wait_ge(count_done, U + 1)
                    dve.wait_ge(relu_done, U + 1)
                    need = U - 1
                    if positive(need):
                        dve.wait_ge(aT_filled, need)
                    dve.scalar_tensor_tensor(act_f[:, par, :], count[:, par, :], 1.0, relu[:, par, :],
                                             ALU.is_equal, ALU.mult).then_inc(act_done, 1)

                def turn(i, last):
                    for u in range(PER):
                        finish(i, u - 3)
                        item(i, u)
                        c, t = divmod(u, ITEMS)
                        if last and c == 1:
                            continue
                        for n in prep_at(t):
                            prep(i, c + 1, n)
                        norm_at(i, c + 1, t)

                dve.wait_ge(gates_ready, 1)
                for n in range(AT_NT):
                    prep(0, 0, n)
                for t in range(STATS_AT, APPLY_AT[-1] + 1):
                    norm_at(0, 0, t)
                dve.wait_ge(consts_hi, 1)
                dve.tensor_tensor(m1_l[:], m1_f[:], m1_h[:], ALU.subtract).then_inc(consts_ready, 1)
                for n in range(AT_NT, AT_LR):
                    prep(0, 0, n)
                dve.wait_ge(consts_hi, 3)
                dve.tensor_tensor(m2_1[DL:2 * DL, :], m2_f[DL:2 * DL, :], m2_2[DL:2 * DL, :], ALU.subtract
                                  ).then_inc(consts_ready, 1)
                dve.wait_ge(zeros_ready, 4)
                prep(0, 0, AT_LR)
                dve.tensor_scalar(b2_g[:], b2_f[:], gate[:, 1, 1:2], None, ALU.mult).then_inc(b2_ready, 1)
                turns(dve, turn)
                lo_part(0, PER * B - 1)
                for u in range(PER * B - 3, PER * B):
                    finish(0, u)

            @block.tensor
            def _(pe):
                def prep(i, c, n):
                    C = 2 * i + c
                    bank = prep_bank(i, c, n)
                    need = n - BANKS + 1 if isinstance(C, int) and C == 0 and n < AT_LR else PREPS * C + n
                    if positive(need):
                        pe.wait_ge(prep_free, need)
                    if n == 0:
                        pe.wait_ge(rows_loaded[c % 2], 16 * LOADS * (i + (c // 2 + 1)))
                        for s in range(ST):
                            last = pe.transpose(bank[:, s * P:(s + 1) * P], den[:, c % 2, s * P:(s + 1) * P], ident[:])
                    elif n < AT_NT:
                        for g in range(GROUPS):
                            last = pe.transpose(bank[:, g * P:(g + 1) * P], heads[:, c % 2, g, (n - AT_X1) * P:(n - AT_X1 + 1) * P],
                                                ident[:])
                    elif n < AT_LR:
                        k = n - AT_NT
                        if k == 0:
                            pe.wait_ge(ln_step, LN_STEPS * (C + 1))
                        for s in range(ST):
                            last = pe.transpose(bank[:, s * P:(s + 1) * P], xn[:, s, k * P:(k + 1) * P], ident[:])
                    else:
                        last = pair_product(pe, bank, lambda k: (m1_h[:, k, :], m1_l[:, k, :]),
                                            lambda k: (xT_h[:, c % 2, k, :], xT_l[:, c % 2, k, :]))
                    last.then_inc(prep_filled, 1)

                def item(i, u):
                    U = PER * i + u
                    c, t = divmod(u, ITEMS)
                    s, q = divmod(t, QT)
                    rows, cols = slice(s * P, (s + 1) * P), slice(q * N, (q + 1) * N)
                    if t == 0:
                        pe.wait_ge(prep_free, PREPS * (2 * i + (c + 1)))
                    need = U - 1
                    if positive(need):
                        pe.wait_ge(is_peak_done, need)
                    logits = banks[:, u % 2, :]
                    pe.matmul(logits, lr_h[:, c, rows], m2_1[:, cols], start=True, stop=False)
                    pe.matmul(logits, lr_l[:, c, rows], m2_2[:, cols], start=False, stop=True
                              ).then_inc(logits_filled, 1)
                    need = U - 1
                    if positive(need):
                        pe.wait_ge(relu_done, need)
                    pair_product(pe, banks[:, 2 + u % 2, :], lambda k: (xT_h[:, c, k, rows], xT_l[:, c, k, rows]),
                                 lambda k: (w1_h[:, k, cols], w1_l[:, k, cols])).then_inc(mid_filled, 1)

                def turn_back(i, u):
                    U = PER * i + u
                    if isinstance(U, int) and U < 0:
                        return
                    pe.wait_ge(act_done, U + 1)
                    need = U - 1
                    if positive(need):
                        pe.wait_ge(aT_lo_done, need)
                    for a in range(RT):
                        last = pe.transpose(banks[:, 4 + u % 2, a * P:(a + 1) * P],
                                            act_f[:, u % 2, a * P:(a + 1) * P], ident[:])
                    last.then_inc(aT_filled, 1)

                def second(i, u):
                    U = PER * i + u
                    if isinstance(U, int) and U < 0:
                        return
                    q = u % QT
                    pe.wait_ge(aT_lo_done, U + 1)
                    if q == 0:
                        need = 2 * ST * i + u // QT
                        if positive(need):
                            pe.wait_ge(result_ready, need)
                    pair_product(pe, banks[:, Y_BANK, :], lambda a: (aT_h[:, u % 2, a, :], aT_l[:, u % 2, a, :]),
                                 lambda a: (w2_h[:, q * RT + a, :], w2_l[:, q * RT + a, :]), range(RT),
                                 start=(q == 0), stop=(q == QT - 1)).then_inc(w2_done, 1)

                def turn(i, last):
                    for u in range(PER):
                        item(i, u)
                        turn_back(i, u - 1)
                        second(i, u - 2)
                        c, t = divmod(u, ITEMS)
                        if last and c == 1:
                            continue
                        for n in prep_at(t):
                            prep(i, c + 1, n)

                for n in range(AT_LR):
                    prep(0, 0, n)
                pe.wait_ge(consts_ready, 1)
                prep(0, 0, AT_LR)
                pe.wait_ge(consts_ready, 2)
                pe.wait_ge(bias_ready, 1)
                turns(pe, turn)
                turn_back(0, PER * B - 1)
                second(0, PER * B - 2)
                second(0, PER * B - 1)


def build(nc, x, ctxT, mask, g_attn, g_ffn, WqT, bq, WkT, bk, WvT, bv, m1, m2, mb, w1, w2, b2, out):
    s_K = [nc.dram_tensor(f"s_K{n}", (B * D, SKV), F16).ap() for n in "hl"]
    s_Q = [nc.dram_tensor(f"s_Q{n}", (B * D, SQ), F16).ap() for n in "hl"]
    s_V = nc.dram_tensor("s_V", (UNITS * SKV, P), F32).ap()
    s_mask = nc.dram_tensor("s_mask", (UNITS, SKV), F16).ap()
    s_ones = nc.dram_tensor("s_ones", (UNITS, N), F16).ap()
    s_heads = nc.dram_tensor("s_heads", (UNITS * QC * P, N), F32).ap()
    s_den = nc.dram_tensor("s_den", (UNITS * QC * HG, N), F32).ap()
    with ExitStack() as ctx:
        ident = ctx.enter_context(nc.sbuf_tensor("ident", [P, P], F32))
        banks = ctx.enter_context(nc.psum_tensor("banks", [P, BANKS, N], F32))
        project(nc, ident, banks, x, ctxT, mask, WqT, WkT, WvT, bq, bk, bv, s_K, s_Q, s_V, s_mask, s_ones)
        w1_h, w1_l = (ctx.enter_context(nc.sbuf_tensor(f"w1_{n}", [P, KT, DFF], F16)) for n in "hl")
        w2_h, w2_l = (ctx.enter_context(nc.sbuf_tensor(f"w2_{n}", [P, FT, D], F16)) for n in "hl")
        ahead = (ctx.enter_context(nc.sbuf_tensor("c_x", [P, 2, ST, D], F32)),
                 ctx.enter_context(nc.sbuf_tensor("c_heads", [P, 2, GROUPS, N], F32)),
                 ctx.enter_context(nc.sbuf_tensor("c_den", [P, 2, N], F32)),
                 [ctx.enter_context(nc.semaphore(f"rows_loaded{i}")) for i in range(2)])
        attend(nc, ident, banks, s_K, s_Q, s_V, s_mask, s_ones, s_heads, s_den, x, ahead, w1, w2, w1_h, w1_l, w2_h, w2_l)
        ffn(nc, ident, banks, x, s_heads, s_den, ahead, g_attn, g_ffn, m1, m2, mb, b2, w1_h, w1_l, w2_h, w2_l, out)


def kernel(x, ctx_1024, mask_BxS2_ik0, g_xattn, g_ffn, L0_xattn_Wq, L0_xattn_bq, L0_xattn_Wk, L0_xattn_bk,
           L0_xattn_Wv, L0_xattn_bv, L0_ffn_m1, L0_ffn_m2, L0_ffn_mb, L0_ffn_w1, L0_ffn_w2, L0_ffn_b2):
    import numpy as _np
    import concourse.bacc as _bacc
    from concourse import mybir as _mybir
    from concourse.bass_utils import run_bass_kernel_spmd as _run

    a = _np.asarray
    laid_out = {
        "x": a(x).reshape(B * SQ, D),
        "ctxT": a(ctx_1024).transpose(0, 2, 1).reshape(B * D, SKV),
        "mask": a(mask_BxS2_ik0).repeat(GROUPS, axis=0),
        "g_attn": a(g_xattn),
        "g_ffn": a(g_ffn),
        "WqT": a(L0_xattn_Wq).T,
        "bq": a(L0_xattn_bq).reshape(KT, P).T,
        "WkT": a(L0_xattn_Wk).T,
        "bk": a(L0_xattn_bk).reshape(KT, P).T,
        "WvT": a(L0_xattn_Wv).T,
        "bv": a(L0_xattn_bv),
        "m1": a(L0_ffn_m1),
        "m2": a(L0_ffn_m2).reshape(DL, DFF),
        "mb": a(L0_ffn_mb).reshape(1, DFF),
        "w1": a(L0_ffn_w1).reshape(D, DFF),
        "w2": a(L0_ffn_w2).transpose(1, 0, 2).reshape(DFF, D),
        "b2": a(L0_ffn_b2),
    }
    nc = _bacc.Bacc("TRN2", target_bir_lowering=False, num_devices=1)
    arrays, args = {}, []
    for name, value in laid_out.items():
        value = _np.ascontiguousarray(value)
        arrays[f"in_{name}"] = value
        args.append(nc.dram_tensor(f"in_{name}", value.shape, _mybir.dt.from_np(value.dtype), kind="ExternalInput").ap())
    out = nc.dram_tensor("out_x", (B * SQ, D), _mybir.dt.float32, kind="ExternalOutput").ap()
    build(nc, *args, out)
    r = _run(nc, [arrays], core_ids=[0])
    return r.results[0]["out_x"].reshape(B, SQ, D)
```
